# Optimizing a Trainium2 kernel written in Bass

```python
import numpy as np
import jax
import jax.numpy as jnp

def _softmax(x, axis=-1):
    return jax.nn.softmax(x, axis=axis)

def _gelu(x):
    return jax.nn.gelu(x, approximate=True)

def _silu(x):
    return jax.nn.silu(x)

def _sigmoid(x):
    return jax.nn.sigmoid(x)

def _layernorm(x, axis=-1, eps=1e-05):
    m = jnp.mean(x, axis=axis, keepdims=True)
    v = jnp.var(x, axis=axis, keepdims=True)
    return (x - m) / jnp.sqrt(v + eps)

def _scatter_add(tgt, idx, src, axis=0):
    return tgt.at[idx].add(src)

def _segment_sum(src, seg, n):
    return jax.ops.segment_sum(src, seg, n)
kernel_name = 'mk_adaln_d1_jaxref_r8_01c4a1'

def setup_inputs(seed: int=0):
    np.random.seed(seed)
    _w = jnp.asarray

    def _L0_attn_setup():
        import math
        import jax, jax.numpy as jnp
        import numpy as np
        IN_F, OUT_F, HID = (512, 512, 512)
        WINDOW, STRIPES = (6, 3)

        def make_sparse_mask(n_in=IN_F, n_out=OUT_F, window=WINDOW, stripes=STRIPES):
            m = np.zeros((n_in, n_out), dtype=np.float32)
            stride = int(math.sqrt(n_in))
            for k in range(stripes):
                ps = stride * k
                for i in range(0, n_in, window):
                    m[ps + i:ps + i + window, i:i + window] = 1.0
            mb = m.astype(bool)
            return jnp.asarray((mb | mb.T).astype(np.float32))
        key = jax.random.key(seed)
        k1, k2, k3, k4 = jax.random.split(key, 4)
        scale = 1.0 / math.sqrt(IN_F)
        x = jax.random.normal(k1, (8, 96, IN_F), dtype=jnp.float32)
        w1 = jax.random.normal(k2, (HID, IN_F), dtype=jnp.float32) * scale
        w2 = jax.random.normal(k3, (OUT_F, HID), dtype=jnp.float32) * scale
        b2 = jax.random.normal(k4, (OUT_F,), dtype=jnp.float32) * scale
        return {'x': x, 'w1': w1, 'w2': w2, 'b2': b2, 'sparse_mask': make_sparse_mask()}
    _L0_attn_in = _L0_attn_setup()

    def _L0_ffn_setup():
        import jax, jax.numpy as jnp
        import numpy as np
        NUM_EXPERTS = 32
        D_MODEL = 512
        TOP_K = 2
        key = jax.random.key(seed)
        k1, k2, k3, k4 = jax.random.split(key, 4)
        x = jax.random.normal(k1, (2, 256, D_MODEL), dtype=jnp.float32)
        gate_w = jax.random.normal(k2, (NUM_EXPERTS, D_MODEL), dtype=jnp.float32) * 0.02
        expert_w = jax.random.normal(k3, (NUM_EXPERTS, D_MODEL, D_MODEL), dtype=jnp.float32) * 0.02
        expert_b = jax.random.normal(k4, (NUM_EXPERTS, D_MODEL), dtype=jnp.float32) * 0.02
        return {'x': x, 'gate_w': gate_w, 'expert_w': expert_w, 'expert_b': expert_b}
    _L0_ffn_in = _L0_ffn_setup()
    _L0_c = _w((lambda *s: np.random.randn(*s).astype(np.float32) * 0.05)(4, 512))
    _L0_wmod = _w((lambda *s: np.random.randn(*s).astype(np.float32) * 0.05)(512, 6 * 512) * 512 ** (-0.5))
    _d = {'L0_attn_x': _L0_attn_in['x'], 'L0_attn_w1': _L0_attn_in['w1'], 'L0_attn_w2': _L0_attn_in['w2'], 'L0_attn_b2': _L0_attn_in['b2'], 'L0_attn_sparse_mask': _L0_attn_in['sparse_mask'], 'L0_ffn_gate_w': _L0_ffn_in['gate_w'], 'L0_ffn_expert_w': _L0_ffn_in['expert_w'], 'L0_ffn_expert_b': _L0_ffn_in['expert_b'], 'L0_c': _L0_c, 'L0_wmod': _L0_wmod}
    _x0 = _d['L0_attn_x']
    _d['L0_attn_x'] = jax.random.normal(jax.random.fold_in(jax.random.key(seed), 1), (4, 256, 512), dtype=_x0.dtype)
    del _x0
    return _d

def reference(L0_attn_x, L0_attn_w1, L0_attn_w2, L0_attn_b2, L0_attn_sparse_mask, L0_ffn_gate_w, L0_ffn_expert_w, L0_ffn_expert_b, L0_c, L0_wmod):

    def _L0_attn_ref(x, w1, w2, b2, sparse_mask):
        import math
        import jax, jax.numpy as jnp
        import numpy as np
        IN_F, OUT_F, HID = (512, 512, 512)
        WINDOW, STRIPES = (6, 3)

        def make_sparse_mask(n_in=IN_F, n_out=OUT_F, window=WINDOW, stripes=STRIPES):
            m = np.zeros((n_in, n_out), dtype=np.float32)
            stride = int(math.sqrt(n_in))
            for k in range(stripes):
                ps = stride * k
                for i in range(0, n_in, window):
                    m[ps + i:ps + i + window, i:i + window] = 1.0
            mb = m.astype(bool)
            return jnp.asarray((mb | mb.T).astype(np.float32))
        attn = jnp.einsum('ds,td->st', w1, w2) * sparse_mask
        y = jnp.einsum('bds,st->bdt', x, attn) + b2
        return jax.nn.gelu(y, approximate=False)

    def _L0_ffn_ref(x, gate_w, expert_w, expert_b):
        import jax, jax.numpy as jnp
        import numpy as np
        NUM_EXPERTS = 32
        D_MODEL = 512
        TOP_K = 2
        B, S, D = x.shape
        T = B * S
        xf = x.reshape(T, D)
        logits = xf @ gate_w.T
        w, idx = jax.lax.top_k(logits, TOP_K)
        w = jax.nn.softmax(w, axis=-1)
        combine = jnp.zeros((T, NUM_EXPERTS), dtype=x.dtype).at[jnp.arange(T)[:, None], idx].add(w)

        def body(acc, params):
            W, b, c = params
            return (acc + c[:, None] * (xf @ W.T + b), None)
        out, _ = jax.lax.scan(body, jnp.zeros_like(xf), (expert_w, expert_b, combine.T))
        return out.reshape(B, S, D)
    x = L0_attn_x
    mod = (_silu(L0_c) @ L0_wmod).reshape(L0_c.shape[0], 6, 1, -1)
    sa, ca, ga, sb, cb, gb = (mod[:, 0], mod[:, 1], mod[:, 2], mod[:, 3], mod[:, 4], mod[:, 5])
    ga = (2 * (ga >= 0) - 1) * jnp.maximum(jnp.abs(ga), 0.25)
    gb = (2 * (gb >= 0) - 1) * jnp.maximum(jnp.abs(gb), 0.25)
    h = _layernorm(x, axis=-1) * (1 + ca) + sa
    x = x + ga * _L0_attn_ref(h, L0_attn_w1, L0_attn_w2, L0_attn_b2, L0_attn_sparse_mask)
    h = _layernorm(x, axis=-1) * (1 + cb) + sb
    x = x + gb * _L0_ffn_ref(h, L0_ffn_gate_w, L0_ffn_expert_w, L0_ffn_expert_b)
    return x

_drawn_inputs = setup_inputs


def setup_inputs(seed=0):
    import zlib

    import numpy as np

    out = dict(_drawn_inputs(seed))
    spreads = {}
    factors = {'L0_attn_b2': 6.971, 'L0_ffn_expert_b': 8.0}
    for name, (base, spread) in spreads.items():
        noise = np.random.default_rng([zlib.crc32(name.encode()), seed]).standard_normal(out[name].shape)
        drawn = base * np.exp(spread * noise) if base else spread * noise
        out[name] = jnp.asarray(drawn.astype(out[name].dtype))
    for name, factor in factors.items():
        out[name] = (out[name] * factor).astype(out[name].dtype)
    return out
```

```python
from contextlib import ExitStack

import concourse.bass as bass
from concourse import mybir

F32 = mybir.dt.float32
F32R = mybir.dt.float32r
I32 = mybir.dt.int32
U32 = mybir.dt.uint32
ALU = mybir.AluOpType
ACT = mybir.ActivationFunctionType
AX_X = mybir.AxisListType.X

P = 128
D = 512
NC = D // P
T = 1024
NT = T // P
NB = 4
PAIR = NT // NB
E = 32
K = 2
NOV = (K * T - 1) // P
NCOL = 48
RING = 8
UNIT = NC * D
FIRST = 8
MODS = {0: 0, 1: 1, 4: 2, 5: 3, 6: 4, 7: 5}
EPS = 1e-5
EMPTY = 4096.0

C_ID, C_TRI, C_ONE, C_IOTA = 0, 128, 256, 384
C_UP, C_INC, C_PID, C_SEL = 512, 512 + E + 1, 512 + 2 * E + 1, 512 + 2 * E + 1 + K * NT
C_ALL = C_SEL + NB * P


def adaln_moe(nc, x, w1, w2t, b2, maskt, gatet, wexp, bexp, ct, wmod, consts, out):
    ctx = ExitStack()
    with ctx:
        def sb(name, shape, dt=F32):
            return ctx.enter_context(nc.sbuf_tensor(name, shape, dt))

        def psum(name, shape):
            return ctx.enter_context(nc.psum_tensor(name, shape, F32))

        def sem(name):
            return ctx.enter_context(nc.semaphore(name))

        h2_rows = nc.dram_tensor("h2_rows", [T, D], F32).ap()
        y_rows = nc.dram_tensor("y_rows", [K * T, D], F32).ap()

        raw = sb("raw", [P, RING, UNIT])
        w_hi = sb("w_hi", [P, 2, NC, D], F32R)
        w_lo = sb("w_lo", [P, 2, NC, D], F32R)
        attn_hi = sb("attn_hi", [P, NC, D], F32R)
        attn_lo = sb("attn_lo", [P, NC, D], F32R)
        ht_hi = sb("ht_hi", [P, NC, PAIR * P], F32R)
        ht_lo = sb("ht_lo", [P, NC, PAIR * P], F32R)
        xs = sb("xs", [P, NT, D])
        norm = sb("norm", [P, PAIR, D])
        act = sb("act", [P, PAIR, D])
        h2 = sb("h2", [P, PAIR, D])
        bc = sb("bc", [P, 4, NB, D])
        g = sb("g", [P, 4, D])
        cst = sb("cst", [P, C_SEL])
        b2_bc = sb("b2_bc", [P, D])
        gate = sb("gate", [P, NC, E])
        c_raw = sb("c_raw", [P, NC, NB])
        c_silu = sb("c_silu", [P, NC, NB])
        c_hi = sb("c_hi", [P, NC, NB], F32R)
        c_lo = sb("c_lo", [P, NC, NB], F32R)
        sel = sb("sel", [NB, NB, P], F32R)
        mod_row = sb("mod_row", [NB, D])
        mod_hi = sb("mod_hi", [NB, D], F32R)
        mod_lo = sb("mod_lo", [NB, D], F32R)
        mod_col = sb("mod_col", [P, 2, NC, NB])
        stats = sb("stats", [P, NT, 6])
        mv = sb("mv", [P, NT, 2])
        rstd = sb("rstd", [P, NT])
        half = sb("half", [P, NT])
        mv2 = sb("mv2", [P, NT, 2])
        rstd2 = sb("rstd2", [P, NT])
        logit = sb("logit", [P, E])
        top = sb("top", [P, NT, 8])
        top_at = sb("top_at", [P, 8], U32)
        top_e = sb("top_e", [P, K, NT])
        hot = sb("hot", [P, K, NT, E])
        before = sb("before", [P, NT + 1, E])
        prod = sb("prod", [P, NT, E])
        place = sb("place", [P, K, NT])
        weight = sb("weight", [P, K, NT])
        w_tmp = sb("w_tmp", [P, 3, NT])
        over_base = sb("over_base", [P, E + 1])
        over_end = sb("over_end", [E, 1])
        over_cmp = sb("over_cmp", [E, 16])
        over_expert = sb("over_expert", [1, 16], I32)
        over_count = sb("over_count", [1, 1], I32)
        slot_w = sb("slot_w", [P, NCOL])
        gather_at = sb("gather_at", [P, NCOL], U32)
        scatter_at = sb("scatter_at", [P, NCOL], U32)
        over_at = sb("over_at", [P, 2], U32)
        sel_raw = h2[0:NB, 0, :]
        mod_tmp = g[0:NB, 2:4, :]
        over_i = act[0:E, 0, 0:2 * P].bitcast(I32).rearrange("p (a m) -> p a m", a=2)
        over = act[0:E, 0, 2 * P:3 * P]
        place_f = act[:, 0, 3 * P:3 * P + 6 * K * NT].rearrange("p (a k n) -> p a k n", a=6, k=K)
        slot_f = act[:, 1, 0:3 * NCOL].rearrange("p (a n) -> p a n", a=3)
        place_i = act[:, 1, 3 * NCOL:3 * NCOL + 4 * K * NT].bitcast(I32).rearrange(
            "p (a k n) -> p a k n", a=4, k=K)
        rank = act[:, 1, 256:256 + NT * E].rearrange("p (n e) -> p n e", n=NT)
        row_hot = norm[:, :, :].rearrange("p a d -> p (a d)").rearrange("p (r m) -> p r m", m=P)
        col_hot = h2[:, :, :].rearrange("p a d -> p (a d)")[:, 0:8 * 2 * NCOL].rearrange(
            "p (r m) -> p r m", m=2 * NCOL)
        share_t = bc[0:E, 0, 0:2, :].rearrange("p a d -> p (a d)")
        b_exp = bc[0:E, 0, 2, :]

        ps_t = psum("ps_t", [P, 4, 512])
        ps_y = psum("ps_y", [P, 2, 512])
        ps_m = psum("ps_m", [P, 2, 512])

        ident = cst[:, C_ID:C_ID + P]
        tri = cst[:, C_TRI:C_TRI + P]
        ones = cst[:, C_ONE:C_ONE + P]
        iota = cst[:, C_IOTA:C_IOTA + P]
        upper = cst[0:E, C_UP:C_UP + E + 1]
        upper_inc = cst[0:E, C_INC:C_INC + E]
        pair_id = cst[:, C_PID:C_PID + K * NT].rearrange("p (k n) -> p k n", k=K)

        consts_landed = sem("consts_landed")
        params_landed = sem("params_landed")
        raw_landed = [sem(f"raw_landed{s}") for s in range(RING)]
        x_landed = [sem(f"x_landed{s}") for s in range(2)]
        mask_landed = sem("mask_landed")
        h2_written = sem("h2_written")
        bexp_landed = sem("bexp_landed")
        silu_done = sem("silu_done")
        c_hi_done = sem("c_hi_done")
        c_lo_done = sem("c_lo_done")
        sel_done = sem("sel_done")
        hi_ready = sem("hi_ready")
        lo_ready = sem("lo_ready")
        m_done = sem("m_done")
        m_read = sem("m_read")
        gains_ready = sem("gains_ready")
        mod_hi_done = sem("mod_hi_done")
        mod_lo_done = sem("mod_lo_done")
        col_ready = sem("col_ready")
        attn_done = sem("attn_done")
        attn_read = sem("attn_read")
        attn_hi_done = sem("attn_hi_done")
        attn_lo_done = sem("attn_lo_done")
        stats_done = sem("stats_done")
        half_done = sem("half_done")
        rstd_done = sem("rstd_done")
        norm_ready = sem("norm_ready")
        t_done = sem("t_done")
        ht_ready = sem("ht_ready")
        ht_hi_done = sem("ht_hi_done")
        ht_lo_done = sem("ht_lo_done")
        y_done = sem("y_done")
        y_read = sem("y_read")
        gelu_done = sem("gelu_done")
        x2_ready = sem("x2_ready")
        stats2_done = sem("stats2_done")
        rstd2_done = sem("rstd2_done")
        h2_scaled = sem("h2_scaled")
        h2_ready = sem("h2_ready")
        t2_done = sem("t2_done")
        h2t_ready = sem("h2t_ready")
        logits_done = sem("logits_done")
        logits_read = sem("logits_read")
        picks_ready = sem("picks_ready")
        ranks_done = sem("ranks_done")
        total_done = sem("total_done")
        over_ready = sem("over_ready")
        base_done = sem("base_done")
        base_read = sem("base_read")
        owner_done = sem("owner_done")
        owner_ready = sem("owner_ready")
        exp_in = sem("exp_in")
        exp_done = sem("exp_done")
        weight_ready = sem("weight_ready")
        place_ready = sem("place_ready")
        row_hot_ready = sem("row_hot_ready")
        col_hot_ready = sem("col_hot_ready")
        table_done = sem("table_done")
        slots_ready = sem("slots_ready")
        share_ready = sem("share_ready")
        share_t_done = sem("share_t_done")
        share_t_read = sem("share_t_read")
        bias_done = sem("bias_done")
        bias_scaled = sem("bias_scaled")
        bias_added = sem("bias_added")
        gathered = [sem(f"gathered{s}") for s in range(4)]
        g_used = sem("g_used")
        xt_hi_done = sem("xt_hi_done")
        xt_lo_done = sem("xt_lo_done")
        expert_done = sem("expert_done")
        expert_read = sem("expert_read")
        scattered = [sem(f"scattered{s}") for s in range(2)]
        ov_w = sem("ov_w")
        ov_at = sem("ov_at")
        ov_g = sem("ov_g")
        ov_t = sem("ov_t")
        ov_hi = sem("ov_hi")
        ov_lo = sem("ov_lo")
        ov_y = sem("ov_y")
        ov_out = sem("ov_out")
        rows_left = sem("rows_left")
        ov_turn = sem("ov_turn")
        ov_done = sem("ov_done")
        rows_complete = sem("rows_complete")
        rows_landed = [sem(f"rows_landed{b}") for b in range(NB)]
        sum_ready = sem("sum_ready")
        out_ready = sem("out_ready")
        stored = sem("stored")
        dve_chain = sem("dve_chain")
        pool_chain = sem("pool_chain")

        def unit_source(j):
            if j in MODS:
                return wmod.rearrange("(p c) n -> p c n", c=NC)[:, :, MODS[j] * D:(MODS[j] + 1) * D]
            return {2: w1, 3: w2t}[j].rearrange("(p c) n -> p c n", c=NC)

        def slot3(s):
            return raw[:, s, :].rearrange("p (c n) -> p c n", c=NC)

        block = ctx.enter_context(nc.Block())

        @block.sync
        def _(sp):
            sp.dma_start(c_raw[:], ct.rearrange("p (c b) -> p c b", c=NC)).then_inc(consts_landed, 16)
            sp.dma_start(cst[:], consts[:, 0:C_SEL]).then_inc(consts_landed, 16)
            sp.dma_start(sel_raw, consts[0:NB, C_SEL:C_ALL]).then_inc(consts_landed, 16)

            def load_unit(j):
                sp.dma_start(slot3(j), unit_source(j)).then_inc(raw_landed[j], 16)

            load_unit(0)
            load_unit(1)
            x_v = x.rearrange("(n p) d -> p n d", p=P)
            for s in range(2):
                n = slice(s * NT // 2, (s + 1) * NT // 2)
                sp.dma_start(xs[:, n, :], x_v[:, n, :]).then_inc(x_landed[s], 16)
            load_unit(2)
            load_unit(3)
            sp.dma_start(g[:], maskt.rearrange("p (c n) -> p c n", c=NC)).then_inc(mask_landed, 16)
            sp.dma_start(b2_bc[:], b2.rearrange("(a n) -> a n", a=1).broadcast_to([P, D])
                         ).then_inc(params_landed, 16)
            sp.dma_start(gate[:], gatet.rearrange("p (c n) -> p c n", c=NC)).then_inc(params_landed, 16)
            for j in range(4, FIRST):
                load_unit(j)

            def load_expert(e, u):
                sp.wait_ge(lo_ready, 2 * e + 2)
                sp.dma_start(raw[:, u, :], wexp[bass.ds(e, 1), :, :].rearrange("a p n -> (a p) n")
                             ).then_inc(raw_landed[u], 16)

            for e in range(RING):
                load_expert(e, e)
            h2_v = h2_rows.rearrange("(b a p) d -> b p a d", p=P, a=PAIR)
            for b in range(NB):
                sp.wait_ge(h2_ready, b + 1)
                sp.dma_start(h2_v[b], h2[:]).then_inc(h2_written, 16)
            with sp.Fori(1, E // RING) as i:
                for u in range(RING):
                    load_expert(i * RING + u, u)

            sp.wait_ge(owner_ready, 2)
            count = sp.value_load(over_count[0:1, 0:1], min_val=0, max_val=NOV)
            sp.wait_ge(lo_ready, 2 * (FIRST + E))
            with sp.Fori(0, NOV) as q:
                with sp.If(count > q):
                    owner = sp.value_load(over_expert[0:1, bass.ds(q, 1)], min_val=0, max_val=E - 1)
                    sp.wait_ge(ov_done, q + 1)
                    sp.dma_start(raw[:, 0, :], wexp[bass.ds(owner, 1), :, :].rearrange("a p n -> (a p) n")
                                 ).then_inc(ov_w, 16)
                with sp.Else():
                    sp.nop()
                sp.nop()
            sp.wait_ge(rows_complete, 1)
            y_v = y_rows.rearrange("(k b a p) d -> b k p a d", p=P, a=PAIR, k=K)
            for b in range(NB):
                for k in range(K):
                    dst = raw[:, b, k * PAIR * D:(k + 1) * PAIR * D].rearrange("p (a d) -> p a d", a=PAIR)
                    sp.dma_start(dst, y_v[b, k]).then_inc(rows_landed[b], 16)
            out_v = out.rearrange("b (a p) d -> b p a d", p=P)
            for b in range(NB):
                sp.wait_ge(out_ready, b + 1)
                sp.dma_start(out_v[b], xs[:, PAIR * b:PAIR * (b + 1), :]).then_inc(stored, 16)
            sp.wait_ge(stored, 16 * NB)

        @block.scalar
        def _(a):
            s = nc.scalar
            a.wait_ge(consts_landed, 3 * 16)
            s.activation(c_silu[:], c_raw[:], ACT.Silu).then_inc(silu_done, 1)
            a.wait_ge(silu_done, 1)
            s.copy(c_hi[:], c_silu[:]).then_inc(c_hi_done, 1)
            s.copy(sel[:], sel_raw.rearrange("p (b m) -> p b m", b=NB)
                   ).then_inc(sel_done, 1)

            def split_hi(src, j2, landed, value):
                a.wait_ge(landed, value)
                for h in range(2):
                    c = slice(2 * h, 2 * h + 2)
                    s.copy(w_hi[:, j2, c, :], src[:, c, :]).then_inc(hi_ready, 1)

            def unit_hi(j):
                split_hi(slot3(j), j % 2, raw_landed[j], 16)

            def read_m(job, dst, src):
                a.wait_ge(m_done, job + 1)
                s.copy(dst, src).then_inc(m_read, 1)

            def read_mod(job):
                read_m(job, mod_row[:], ps_m[0:NB, job % 2, :])

            def mod_split_hi(n):
                if n % 3 == 0:
                    a.wait_ge(gains_ready, n // 3 + 1)
                else:
                    a.wait_ge(m_read, {1: 6, 2: 15}[n])
                if n > 0:
                    a.wait_ge(m_done, {1: 10, 2: 14, 3: 20}[n])
                s.copy(mod_hi[:], mod_row[:]).then_inc(mod_hi_done, 1)

            def read_bc(n, job0):
                for b in range(NB):
                    read_m(job0 + b, bc[:, n, b, :], ps_m[:, (job0 + b) % 2, :])

            def modulate(b):
                a.wait_ge(t_done, b + 1)
                if b == 0:
                    a.wait_ge(col_ready, 1)
                nt = norm[:, :, :].rearrange("p a d -> p (a d)").rearrange("p (c m) -> p c m", c=NC)
                for c in range(NC):
                    s.activation(nt[:, c, :], ps_t[:, c // 2, (c % 2) * 256:(c % 2) * 256 + 256],
                                 ACT.Identity, bias=mod_col[:, 0, c, b:b + 1],
                                 scale=mod_col[:, 1, c, b:b + 1]).then_inc(ht_ready, 1)
                if b >= 1:
                    a.wait_ge(y_done, PAIR * b)
                a.wait_ge(ht_ready, NC * (b + 1))
                s.copy(ht_hi[:], nt).then_inc(ht_hi_done, 1)

            def gelu(b):
                for t in range(PAIR):
                    a.wait_ge(y_read, PAIR * b + t + 1)
                    s.activation(act[:, t, :], act[:, t, :], ACT.Gelu).then_inc(gelu_done, 1)

            def copy_h2t(n):
                a.wait_ge(t2_done, n + 1)
                if n >= 2:
                    a.wait_ge(logits_done, n - 1)
                s.copy(g[:, n % 2, :], ps_t[:, 2 + n % 2, :]).then_inc(h2t_ready, 1)

            unit_hi(0)
            unit_hi(1)
            read_mod(0)
            read_m(1, mod_col[:, 0, :, :].rearrange("p c b -> p (c b)"), ps_m[:, 1, 0:NC * NB])
            a.wait_ge(m_done, 2)
            read_mod(2)
            read_m(3, mod_col[:, 1, :, :].rearrange("p c b -> p (c b)"), ps_m[:, 1, 0:NC * NB])
            unit_hi(2)
            unit_hi(3)
            for c in range(NC):
                a.wait_ge(attn_read, c + 1)
                s.copy(attn_hi[:, c, :], h2[:, c % 2, :]).then_inc(attn_hi_done, 1)
            modulate(0)
            a.wait_ge(attn_done, NC)
            unit_hi(4)
            unit_hi(5)
            read_mod(4)
            mod_split_hi(0)
            a.wait_ge(m_done, 5)
            unit_hi(6)
            modulate(1)
            a.wait_ge(mod_lo_done, 1)
            read_mod(5)
            unit_hi(7)
            gelu(0)
            read_bc(0, 6)
            mod_split_hi(1)
            read_bc(1, 10)
            a.wait_ge(mod_lo_done, 2)
            read_mod(14)
            mod_split_hi(2)
            modulate(2)
            gelu(1)
            a.wait_ge(mod_lo_done, 3)
            read_mod(15)
            read_bc(2, 16)
            mod_split_hi(3)
            modulate(3)
            read_bc(3, 20)
            copy_h2t(0)
            copy_h2t(1)
            gelu(2)

            def expert_hi(e0, u):
                if isinstance(e0, int) and e0 + u < 2:
                    a.wait_ge(m_done, 15 + u)
                else:
                    a.wait_ge(expert_done, e0 + u)
                a.wait_ge(raw_landed[u % RING], e0 * 2 + 16 * (2 + u // RING))
                for h in range(2):
                    c = slice(2 * h, 2 * h + 2)
                    s.copy(w_hi[:, u % 2, c, :], slot3(u % RING)[:, c, :]).then_inc(hi_ready, 1)

            expert_hi(0, 0)
            expert_hi(0, 1)
            copy_h2t(2)
            copy_h2t(3)
            gelu(3)
            a.wait_ge(x2_ready, PAIR * NB)
            a.dma_start(b_exp, bexp).then_inc(bexp_landed, 16)
            for n in range(4, NT):
                copy_h2t(n)
            a.wait_ge(exp_in, 1)
            s.activation(w_tmp[:, 1, :], w_tmp[:, 0, :], ACT.Exp).then_inc(exp_done, 1)
            for h in range(2):
                a.wait_ge(share_t_done, h + 1)
                s.copy(share_t[:, h * 512:(h + 1) * 512], ps_t[0:E, 2 + h, :]).then_inc(share_t_read, 1)

            def rows_hi(e0, u):
                a.wait_ge(g_used, e0 + u + 1)
                a.wait_ge(expert_done, e0 + u)
                k = u % 2
                s.copy(ht_hi[:, :, k * P:(k + 1) * P], ps_t[:, k, :].rearrange("p (c m) -> p c m", c=NC)
                       ).then_inc(xt_hi_done, 1)

            def rows_out(e0, u):
                a.wait_ge(expert_done, e0 + u + 2)
                a.wait_ge(rows_left, e0 + u + 1)
                s.activation(act[:, u % 2, :], ps_m[:, u % 2, :], ACT.Copy,
                             scale=slot_w[:, bass.ds(e0 + u, 1)]).then_inc(expert_read, 1)

            def step(e0, u, last=False):
                rows_hi(e0, u + 1)
                rows_out(e0, u)
                if not (last and u >= RING - 2):
                    expert_hi(e0, u + 2)

            a.wait_ge(slots_ready, 3)
            a.wait_ge(g_used, 1)
            s.copy(ht_hi[:, :, 0:P], ps_t[:, 0, :].rearrange("p (c m) -> p c m", c=NC)
                   ).then_inc(xt_hi_done, 1)
            with a.Fori(0, E // RING - 1) as i:
                for u in range(RING):
                    step(i * RING, u)
            for u in range(RING):
                step(E - RING, u, last=True)

            count = a.value_load(over_count[0:1, 0:1], min_val=0, max_val=NOV)
            with a.Fori(0, NOV) as q:
                with a.If(count > q):
                    a.wait_ge(ov_w, 16 * q + 16)
                    s.copy(w_hi[:, 0, :, :], slot3(0)).then_inc(ov_hi, 1)
                    a.wait_ge(ov_t, q + 1)
                    s.copy(ht_hi[:, :, 0:P], ps_t[:, 0, :].rearrange("p (c m) -> p c m", c=NC)
                           ).then_inc(ov_hi, 1)
                    a.wait_ge(ov_y, q + 1)
                    s.activation(act[:, 0, :], ps_m[:, 0, :], ACT.Copy, scale=slot_w[:, bass.ds(q + E, 1)]
                                 ).then_inc(ov_out, 1)
                with a.Else():
                    a.nop()
                a.nop()

        @block.vector
        def _(v):
            d = nc.vector
            linked = [0]

            def link(ins):
                linked[0] += 1
                ins.then_inc(dve_chain, 1)
                v.wait_ge(dve_chain, linked[0])

            def unit_lo(j):
                for h in range(2):
                    c = slice(2 * h, 2 * h + 2)
                    v.wait_ge(hi_ready, 2 * j + h + 1)
                    d.tensor_tensor(w_lo[:, j % 2, c, :], slot3(j)[:, c, :],
                                    w_hi[:, j % 2, c, :].bitcast(F32), ALU.subtract).then_inc(lo_ready, 1)

            def norm_stats(src, st, m, n, done):
                link(d.bn_stats(st[:, n, :], src))
                d.bn_aggr(m[:, n, :], st[:, n, :]).then_inc(done, 1)

            def norm_rows(b):
                if b >= 1:
                    v.wait_ge(ht_lo_done, b)
                    v.wait_ge(ht_hi_done, b)
                for t in range(PAIR):
                    n = PAIR * b + t
                    d.tensor_scalar(norm[:, t, :], xs[:, n, :], mv[:, n, 0:1], rstd[:, n:n + 1],
                                    ALU.subtract, ALU.mult).then_inc(norm_ready, 1)

            def ht_lo_part(b):
                v.wait_ge(ht_hi_done, b + 1)
                nt = norm[:, :, :].rearrange("p a d -> p (a d)").rearrange("p (c m) -> p c m", c=NC)
                d.tensor_tensor(ht_lo[:], nt, ht_hi[:].bitcast(F32), ALU.subtract).then_inc(ht_lo_done, 1)

            def add_b2(b):
                for t in range(PAIR):
                    v.wait_ge(y_done, PAIR * b + t + 1)
                    if b >= 1:
                        v.wait_ge(x2_ready, 2 * b)
                    d.tensor_tensor(act[:, t, :], ps_y[:, t, :], b2_bc[:], ALU.add).then_inc(y_read, 1)

            def bound_gain(n, job):
                v.wait_ge(m_read, job + 1)
                link(d.tensor_scalar(mod_tmp[:, 0, :], mod_row[:], 0.0, 2.0, ALU.is_ge, ALU.mult))
                link(d.tensor_scalar(mod_tmp[:, 0, :], mod_tmp[:, 0, :], -1.0, None, ALU.add))
                link(d.scalar_tensor_tensor(out=mod_tmp[:, 1, :], in0=mod_row[:], scalar=-1.0,
                                            in1=mod_row[:], op0=ALU.mult, op1=ALU.max))
                d.scalar_tensor_tensor(out=mod_row[:], in0=mod_tmp[:, 1, :], scalar=0.25,
                                       in1=mod_tmp[:, 0, :], op0=ALU.max, op1=ALU.mult
                                       ).then_inc(gains_ready, 1)

            def mod_lo_part(n):
                v.wait_ge(mod_hi_done, n + 1)
                d.tensor_tensor(mod_lo[:], mod_row[:], mod_hi[:].bitcast(F32), ALU.subtract
                                ).then_inc(mod_lo_done, 1)

            def second_norm(b):
                v.wait_ge(x2_ready, 2 * b + 2)
                for t in range(PAIR):
                    norm_stats(xs[:, PAIR * b + t, :], stats, mv2, PAIR * b + t, stats2_done)

            def scale_rows(b):
                v.wait_ge(rstd2_done, b + 1)
                if b == 0:
                    v.wait_ge(attn_lo_done, NC)
                else:
                    v.wait_ge(t2_done, PAIR * b)
                    v.wait_ge(h2_written, 16 * b)
                v.wait_ge(m_read, 20)
                for t in range(PAIR):
                    n = PAIR * b + t
                    link(d.tensor_scalar(h2[:, t, :], xs[:, n, :], mv2[:, n, 0:1], rstd2[:, n:n + 1],
                                         ALU.subtract, ALU.mult))
                    d.scalar_tensor_tensor(out=h2[:, t, :], in0=bc[:, 2, b, :], scalar=1.0,
                                           in1=h2[:, t, :], op0=ALU.add, op1=ALU.mult
                                           ).then_inc(h2_scaled, 1)

            def pick(n):
                v.wait_ge(logits_done, n + 1)
                d.tensor_copy(logit[:], ps_m[:, 0, 0:E]).then_inc(logits_read, 1)
                v.wait_ge(logits_read, n + 1)
                link(d.max(top[:, n, :], logit[:]))
                link(d.max_index(top_at[:], top[:, n, :], logit[:]))
                link(d.tensor_copy(top_e[:, :, n], top_at[:, 0:K]))
                for k in range(K):
                    ins = d.tensor_scalar(hot[:, k, n, :], iota[:, 0:E], top_e[:, k, n:n + 1], None,
                                          ALU.is_equal)
                    link(ins)
                link(d.tensor_tensor(prod[:, n, :], hot[:, 0, n, :], hot[:, 1, n, :], ALU.add))
                d.tensor_tensor(before[:, n + 1, :], before[:, n, :], prod[:, n, :], ALU.add
                                ).then_inc(picks_ready, 1)
                v.wait_ge(picks_ready, n + 1)

            v.wait_ge(c_hi_done, 1)
            d.tensor_tensor(c_lo[:], c_silu[:], c_hi[:].bitcast(F32), ALU.subtract).then_inc(c_lo_done, 1)
            link(d.memset(before[:, 0, :], 0.0))
            unit_lo(0)
            unit_lo(1)
            for n in range(NT):
                if n % (NT // 2) == 0:
                    v.wait_ge(x_landed[n // (NT // 2)], 16)
                norm_stats(xs[:, n, :], stats, mv, n, stats_done)
            unit_lo(2)
            unit_lo(3)
            v.wait_ge(rstd_done, 2)
            norm_rows(0)
            v.wait_ge(m_read, 4)
            d.tensor_scalar(mod_col[:, 1, :, :], mod_col[:, 1, :, :], 1.0, None, ALU.add
                            ).then_inc(col_ready, 1)

            def mask_attn(c):
                v.wait_ge(attn_done, c + 1)
                d.tensor_tensor(h2[:, c % 2, :], ps_t[:, c, :], g[:, c, :], ALU.mult).then_inc(attn_read, 1)

            def attn_lo_part(c):
                v.wait_ge(attn_hi_done, c + 1)
                d.tensor_tensor(attn_lo[:, c, :], h2[:, c % 2, :], attn_hi[:, c, :].bitcast(F32),
                                ALU.subtract).then_inc(attn_lo_done, 1)

            v.wait_ge(mask_landed, 16)
            v.wait_ge(sel_done, 1)
            mask_attn(0)
            mask_attn(1)
            for c in range(2, NC):
                attn_lo_part(c - 2)
                v.wait_ge(attn_lo_done, c - 1)
                mask_attn(c)
            attn_lo_part(NC - 2)
            attn_lo_part(NC - 1)
            ht_lo_part(0)
            unit_lo(4)
            unit_lo(5)
            norm_rows(1)
            v.wait_ge(params_landed, 2 * 16)
            add_b2(0)
            bound_gain(0, 4)
            v.wait_ge(gains_ready, 1)
            mod_lo_part(0)
            unit_lo(6)
            ht_lo_part(1)
            unit_lo(7)
            norm_rows(2)
            mod_lo_part(1)
            mod_lo_part(2)
            second_norm(0)
            ht_lo_part(2)
            add_b2(1)
            norm_rows(3)
            bound_gain(3, 15)
            v.wait_ge(gains_ready, 2)
            mod_lo_part(3)
            scale_rows(0)
            ht_lo_part(3)
            second_norm(1)
            add_b2(2)
            scale_rows(1)
            pick(0)
            pick(1)

            def expert_lo(e0, u):
                for h in range(2):
                    c = slice(2 * h, 2 * h + 2)
                    v.wait_ge(hi_ready, e0 * 2 + 2 * (FIRST + u) + h + 1)
                    d.tensor_tensor(w_lo[:, u % 2, c, :], slot3(u % RING)[:, c, :],
                                    w_hi[:, u % 2, c, :].bitcast(F32), ALU.subtract).then_inc(lo_ready, 1)

            expert_lo(0, 0)
            expert_lo(0, 1)
            second_norm(2)
            add_b2(3)
            scale_rows(2)
            pick(2)
            pick(3)
            second_norm(3)
            scale_rows(3)
            for n in range(4, NT):
                pick(n)

            d.tensor_tensor(w_tmp[:, 0, :], top[:, :, 1], top[:, :, 0], ALU.subtract).then_inc(exp_in, 1)
            v.wait_ge(total_done, 1)
            link(d.tensor_scalar(over_i[:, 0, :], ps_m[0:E, 0, 0:P], float(P - 1), None, ALU.add))
            link(d.tensor_scalar(over_i[:, 1, :], over_i[:, 0, :], 7, None, ALU.arith_shift_right))
            d.tensor_scalar(over[:], over_i[:, 1, :], -1.0, 0.0, ALU.add, ALU.max).then_inc(over_ready, 1)
            v.wait_ge(exp_done, 1)
            link(d.tensor_scalar(w_tmp[:, 2, :], w_tmp[:, 1, :], 1.0, None, ALU.add))
            link(d.reciprocal(weight[:, 0, :], w_tmp[:, 2, :]))
            d.tensor_tensor(weight[:, 1, :], w_tmp[:, 1, :], weight[:, 0, :], ALU.mult
                            ).then_inc(weight_ready, 1)
            v.wait_ge(base_done, 1)
            d.tensor_copy(over_base[:], ps_m[:, 0, 0:E + 1]).then_inc(base_read, 1)
            d.tensor_copy(over_end[:], ps_m[0:E, 0, 64:65]).then_inc(base_read, 1)
            v.wait_ge(base_read, 2)
            v.wait_ge(ranks_done, NT)
            base = over_base[:, 0:E].unsqueeze(1).broadcast_to([P, NT, E])
            link(d.scalar_tensor_tensor(out=rank[:], in0=base, scalar=float(T),
                                        in1=ps_m[:, 1, 0:NT * E].rearrange("p (n e) -> p n e", n=NT),
                                        op0=ALU.mult, op1=ALU.add))
            for k in range(K):
                link(d.tensor_tensor(prod[:], rank[:], hot[:, k, :, :], ALU.mult))
                link(d.tensor_reduce(place[:, k, :], prod[:], AX_X, ALU.add))
            BOTH, RANK, OVER, ROW = range(4)
            link(d.tensor_copy(place_i[:, BOTH], place[:]))
            d.tensor_scalar(place_i[:, RANK], place_i[:, BOTH], T - 1, 7, ALU.bitwise_and,
                            ALU.arith_shift_right)
            d.tensor_scalar(place_i[:, OVER], place_i[:, BOTH], 10, None, ALU.arith_shift_right)
            link(d.tensor_scalar(place_i[:, ROW], place_i[:, BOTH], P - 1, None, ALU.bitwise_and))
            f_chunk, f_over, f_row, f_is, f_col, f_sum = (place_f[:, i] for i in range(6))
            d.tensor_copy(f_chunk, place_i[:, RANK])
            d.tensor_copy(f_over, place_i[:, OVER])
            link(d.tensor_copy(f_row, place_i[:, ROW]))
            link(d.tensor_scalar(f_is, f_chunk, 1.0, None, ALU.is_ge))
            link(d.scalar_tensor_tensor(out=f_sum, in0=f_chunk, scalar=float(E - 1), in1=f_over,
                                        op0=ALU.add, op1=ALU.add))
            link(d.tensor_tensor(f_sum, f_sum, top_e[:], ALU.subtract))
            link(d.tensor_tensor(f_sum, f_sum, f_is, ALU.mult))
            d.tensor_tensor(f_col, f_sum, top_e[:], ALU.add).then_inc(place_ready, 1)
            v.wait_ge(place_ready, 1)
            for r in range(K * NT):
                if r >= 8:
                    v.wait_ge(table_done, r - 7)
                k, n = divmod(r, NT)
                d.tensor_scalar(row_hot[:, r % 8, :], iota, place_f[:, 2, k, n:n + 1], None, ALU.is_equal
                                ).then_inc(row_hot_ready, 1)
            v.wait_ge(table_done, K * NT)
            d.tensor_copy(slot_w[:], ps_t[:, 0, NCOL:2 * NCOL]).then_inc(slots_ready, 1)
            link(d.tensor_scalar(slot_f[:, 0, :], ps_t[:, 0, 0:NCOL], 0.0, EMPTY, ALU.is_equal, ALU.mult))
            link(d.scalar_tensor_tensor(out=slot_f[:, 1, :], in0=ps_t[:, 0, 0:NCOL], scalar=-1.0,
                                        in1=slot_f[:, 0, :], op0=ALU.add, op1=ALU.add))
            link(d.tensor_scalar(slot_f[:, 2, :], slot_f[:, 1, :], float(T), -float(T), ALU.is_ge,
                                 ALU.mult))
            d.tensor_tensor(gather_at[:], slot_f[:, 1, :], slot_f[:, 2, :], ALU.add).then_inc(slots_ready, 1)
            d.tensor_copy(scatter_at[:], slot_f[:, 1, :]).then_inc(slots_ready, 1)
            link(d.tensor_scalar(over_cmp[:], iota[0:E, 0:16], over_end[:, 0:1], None, ALU.is_ge))
            d.tensor_copy(over_count[:], over_base[0:1, E:E + 1]).then_inc(owner_ready, 1)
            v.wait_ge(owner_done, 1)
            d.tensor_scalar(over_expert[:], ps_m[0:1, 0, 0:16], float(E - 1), None, ALU.min
                            ).then_inc(owner_ready, 1)

            def rows_lo(e0, u):
                v.wait_ge(xt_hi_done, e0 + u + 1)
                k = u % 2
                d.tensor_tensor(ht_lo[:, :, k * P:(k + 1) * P],
                                ps_t[:, k, :].rearrange("p (c m) -> p c m", c=NC),
                                ht_hi[:, :, k * P:(k + 1) * P].bitcast(F32), ALU.subtract
                                ).then_inc(xt_lo_done, 1)

            rows_lo(0, 0)
            for n in range(NT):
                v.wait_ge(bias_done, n + 1)
                if n >= 4:
                    v.wait_ge(bias_added, n - 3)
                d.tensor_tensor(bc[:, 1, n % 4, :], ps_y[:, n % 2, :], bc[:, 3, n // PAIR, :], ALU.mult
                                ).then_inc(bias_scaled, 1)

            def step(e0, u, last=False):
                rows_lo(e0, u + 1)
                if not (last and u >= RING - 2):
                    expert_lo(e0, u + 2)

            with v.Fori(0, E // RING - 1) as i:
                for u in range(RING):
                    step(i * RING, u)
            for u in range(RING):
                step(E - RING, u, last=True)

            count = v.value_load(over_count[0:1, 0:1], min_val=0, max_val=NOV)
            with v.Fori(0, NOV) as q:
                with v.If(count > q):
                    v.wait_ge(ov_hi, 2 * q + 1)
                    d.tensor_tensor(w_lo[:, 0, :, :], slot3(0), w_hi[:, 0, :, :].bitcast(F32),
                                    ALU.subtract).then_inc(ov_lo, 1)
                    v.wait_ge(ov_hi, 2 * q + 2)
                    d.tensor_tensor(ht_lo[:, :, 0:P], ps_t[:, 0, :].rearrange("p (c m) -> p c m", c=NC),
                                    ht_hi[:, :, 0:P].bitcast(F32), ALU.subtract).then_inc(ov_lo, 1)
                with v.Else():
                    v.nop()
                v.nop()

            for b in range(NB):
                v.wait_ge(rows_landed[b], 16 * K)
                r = raw[:, b, :].rearrange("p (k a d) -> p k a d", k=K, a=PAIR)
                link(d.tensor_tensor(r[:, 0], r[:, 0], r[:, 1], ALU.add))
                for t in range(PAIR):
                    ins = d.tensor_tensor(r[:, 0, t, :], r[:, 0, t, :], bc[:, 3, b, :], ALU.mult)
                ins.then_inc(sum_ready, 1)

        @block.gpsimd
        def _(p):
            q7 = nc.gpsimd
            p.sem_inc(expert_done, 1)
            p.sem_inc(expert_read, 2)
            p.sem_inc(rows_left, 2)
            p.sem_inc(ov_done, 1)
            q7.memset(half[:], -0.5).then_inc(half_done, 1)
            p.wait_ge(half_done, 1)

            chained = [0]

            def link(ins):
                chained[0] += 1
                ins.then_inc(pool_chain, 1)
                p.wait_ge(pool_chain, chained[0])

            def power(m, out_, n0, n1, done):
                link(q7.tensor_scalar(out_[:, n0:n1], m[:, n0:n1, 1], EPS, None, ALU.add))
                q7.tensor_tensor(out_[:, n0:n1], out_[:, n0:n1], half[:, n0:n1], ALU.pow).then_inc(done, 1)

            p.wait_ge(stats_done, NT // 2)
            power(mv, rstd, 0, NT // 2, rstd_done)
            p.wait_ge(stats_done, NT)
            power(mv, rstd, NT // 2, NT, rstd_done)

            def add_attn(b):
                for t in range(PAIR):
                    n = PAIR * b + t
                    p.wait_ge(gelu_done, n + 1)
                    if n == 0:
                        p.wait_ge(m_read, 10)
                    link(q7.tensor_tensor(act[:, t, :], act[:, t, :], bc[:, 0, b, :], ALU.mult))
                    q7.tensor_tensor(xs[:, n, :], xs[:, n, :], act[:, t, :], ALU.add).then_inc(x2_ready, 1)

            def shift_rows(b):
                p.wait_ge(stats2_done, PAIR * (b + 1))
                power(mv2, rstd2, PAIR * b, PAIR * (b + 1), rstd2_done)
                p.wait_ge(h2_scaled, PAIR * (b + 1))
                link(q7.tensor_tensor(h2[:, 0, :], h2[:, 0, :], bc[:, 1, b, :], ALU.add))
                q7.tensor_tensor(h2[:, 1, :], h2[:, 1, :], bc[:, 1, b, :], ALU.add).then_inc(h2_ready, 1)

            for b in range(NB):
                add_attn(b)
                shift_rows(b)

            p.wait_ge(weight_ready, 1)
            p.wait_ge(place_ready, 1)
            for r in range(K * NT):
                k, n = divmod(r, NT)
                if r == 0:
                    p.wait_ge(h2_written, 16 * NB)
                if r >= 8:
                    p.wait_ge(table_done, r - 7)
                for half_, val in ((0, pair_id), (1, weight)):
                    ins = q7.tensor_scalar(col_hot[:, r % 8, half_ * NCOL:(half_ + 1) * NCOL],
                                           iota[:, 0:NCOL], place_f[:, 4, k, n:n + 1],
                                           val[:, k, n:n + 1], ALU.is_equal, ALU.mult)
                    ins.then_inc(col_hot_ready, 1)

            def gather(at, s, done):
                q7.indirect_dma_start(g[:, s, :], None, h2_rows,
                                      bass.IndirectOffsetOnAxis(ap=at, axis=0),
                                      bounds_check=T - 1, oob_is_err=False).then_inc(done, 16)

            def scatter(at, s, done):
                q7.indirect_dma_start(y_rows, bass.IndirectOffsetOnAxis(ap=at, axis=0), act[:, s, :], None,
                                      bounds_check=K * T - 1, oob_is_err=False).then_inc(done, 16)

            p.wait_ge(slots_ready, 3)
            p.wait_ge(logits_done, NT)
            for s in range(3):
                gather(gather_at[:, s:s + 1], s, gathered[s])

            w0 = weight[:, 0, :].unsqueeze(2).broadcast_to([P, NT, E])
            w1_ = weight[:, 1, :].unsqueeze(2).broadcast_to([P, NT, E])
            link(q7.tensor_tensor(prod[:], hot[:, 0], w0, ALU.mult))
            link(q7.tensor_tensor(rank[:], hot[:, 1], w1_, ALU.mult))
            q7.tensor_tensor(prod[:], prod[:], rank[:], ALU.add).then_inc(share_ready, 1)
            for n in range(NT):
                p.wait_ge(bias_scaled, n + 1)
                q7.tensor_tensor(xs[:, n, :], xs[:, n, :], bc[:, 1, n % 4, :], ALU.add
                                 ).then_inc(bias_added, 1)

            for e in range(E):
                p.wait_ge(g_used, e + 1)
                gather(gather_at[:, e + 3:e + 4], (e + 3) % 4, gathered[(e + 3) % 4])
                if e >= 1:
                    p.wait_ge(scattered[(e - 1) % 2], 16 * ((e - 1) // 2 + 1))
                    p.sem_inc(rows_left, 1)
                p.wait_ge(expert_read, e + 3)
                scatter(scatter_at[:, e:e + 1], e % 2, scattered[e % 2])

            p.wait_ge(owner_ready, 2)
            count = p.value_load(over_count[0:1, 0:1], min_val=0, max_val=NOV)
            for s in range(2):
                p.wait_ge(scattered[s], 16 * (E // 2))
            for s in range(3):
                p.wait_ge(gathered[s], 16 * (E // 4 + 1))
            with p.Fori(0, NOV) as q:
                with p.If(count > q):
                    q7.tensor_copy(over_at[:, 0:1], gather_at[:, bass.ds(q + E, 1)]).then_inc(ov_at, 1)
                    q7.tensor_copy(over_at[:, 1:2], scatter_at[:, bass.ds(q + E, 1)]).then_inc(ov_at, 1)
                    p.wait_ge(ov_at, 2 * q + 2)
                    p.sem_inc(ov_turn, 1)
                    gather(over_at[:, 0:1], 3, ov_g)
                    p.wait_ge(ov_out, q + 1)
                    p.sem_inc(ov_turn, 1)
                    scatter(over_at[:, 1:2], 0, scattered[0])
                    p.wait_ge(scattered[0], 16 * q + 16 * (E // 2 + 1))
                    p.sem_inc(ov_done, 1)
                with p.Else():
                    p.nop()
                p.nop()
            p.sem_inc(rows_complete, 1)

            p.wait_ge(bias_added, NT)
            for b in range(NB):
                p.wait_ge(sum_ready, b + 1)
                r = raw[:, b, :].rearrange("p (k a d) -> p k a d", k=K, a=PAIR)
                q7.tensor_tensor(xs[:, PAIR * b:PAIR * (b + 1), :], xs[:, PAIR * b:PAIR * (b + 1), :],
                                 r[:, 0], ALU.add).then_inc(out_ready, 1)

        @block.tensor
        def _(pe):
            t_ = nc.tensor

            def product(out_, l_hi, l_lo, r_hi, r_lo):
                for c in range(NC):
                    t_.matmul(out_, l_hi(c), r_hi(c), start=(c == 0), stop=False)
                    t_.matmul(out_, l_hi(c), r_lo(c), start=False, stop=False)
                    ins = t_.matmul(out_, l_lo(c), r_hi(c), start=False, stop=(c == NC - 1))
                return ins

            def mod_unit(j, job):
                pe.wait_ge(lo_ready, 2 * j + 2)
                if job >= 2:
                    pe.wait_ge(m_read, job - 1)
                product(ps_m[0:NB, job % 2, :], lambda c: c_hi[:, c, :], lambda c: c_lo[:, c, :],
                        lambda c: w_hi[:, j % 2, c, :], lambda c: w_lo[:, j % 2, c, :]).then_inc(m_done, 1)

            def mod_columns(job):
                pe.wait_ge(m_read, job)
                for c in range(NC):
                    ins = t_.transpose(ps_m[:, job % 2, c * NB:(c + 1) * NB], mod_row[:, c * P:(c + 1) * P],
                                       ident[0:NB, 0:NB])
                ins.then_inc(m_done, 1)

            def broadcast(n, job0):
                pe.wait_ge(mod_lo_done, n + 1)
                for b in range(NB):
                    job = job0 + b
                    pe.wait_ge(m_read, job - 1)
                    t_.matmul(ps_m[:, job % 2, :], sel[:, b, :], mod_hi[:], start=True, stop=False)
                    t_.matmul(ps_m[:, job % 2, :], sel[:, b, :], mod_lo[:], start=False, stop=True
                              ).then_inc(m_done, 1)

            def transpose_pair(b):
                pe.wait_ge(norm_ready, PAIR * (b + 1))
                if b == 0:
                    pe.wait_ge(attn_read, NC)
                else:
                    pe.wait_ge(ht_ready, NC * b)
                for c in range(NC):
                    for t in range(PAIR):
                        ins = t_.transpose(ps_t[:, c // 2, (c % 2) * 256 + t * P:(c % 2) * 256 + (t + 1) * P],
                                           norm[:, t, c * P:(c + 1) * P], ident)
                ins.then_inc(t_done, 1)

            def attention(b):
                pe.wait_ge(ht_lo_done, b + 1)
                if b == 0:
                    pe.wait_ge(attn_lo_done, NC)
                for t in range(PAIR):
                    if b >= 1:
                        pe.wait_ge(y_read, PAIR * (b - 1) + t + 1)
                    m = slice(t * P, (t + 1) * P)
                    product(ps_y[:, t, :], lambda c: ht_hi[:, c, m], lambda c: ht_lo[:, c, m],
                            lambda c: attn_hi[:, c, :], lambda c: attn_lo[:, c, :]).then_inc(y_done, 1)

            def gating(b):
                pe.wait_ge(h2_ready, b + 1)
                for t in range(PAIR):
                    n = PAIR * b + t
                    if n >= 2:
                        pe.wait_ge(h2t_ready, n - 1)
                    for c in range(NC):
                        ins = t_.transpose(ps_t[:, 2 + t, c * P:(c + 1) * P], h2[:, t, c * P:(c + 1) * P],
                                           ident)
                    ins.then_inc(t2_done, 1)
                for t in range(PAIR):
                    n = PAIR * b + t
                    pe.wait_ge(h2t_ready, n + 1)
                    if n == 0:
                        pe.wait_ge(m_read, 24)
                    else:
                        pe.wait_ge(logits_read, n)
                    for c in range(NC):
                        ins = t_.matmul(ps_m[:, 0, 0:E], g[:, n % 2, c * P:(c + 1) * P], gate[:, c, :],
                                        start=(c == 0), stop=(c == NC - 1))
                    ins.then_inc(logits_done, 1)

            def ranks(n):
                pe.wait_ge(picks_ready, n + 1)
                o = ps_m[:, 1, n * E:(n + 1) * E]
                t_.matmul(o, tri, prod[:, n, :], start=True, stop=False)
                t_.matmul(o, ones, before[:, n, :], start=False, stop=True).then_inc(ranks_done, 1)

            pe.wait_ge(c_lo_done, 1)
            mod_unit(0, 0)
            mod_columns(1)
            mod_unit(1, 2)
            mod_columns(3)
            pe.wait_ge(lo_ready, 2 * 4)
            for c in range(NC):
                m = slice(c * P, (c + 1) * P)
                product(ps_t[:, c, :], lambda q: w_hi[:, 0, q, m], lambda q: w_lo[:, 0, q, m],
                        lambda q: w_hi[:, 1, q, :], lambda q: w_lo[:, 1, q, :]).then_inc(attn_done, 1)
            transpose_pair(0)
            attention(0)
            mod_unit(4, 4)
            transpose_pair(1)
            mod_unit(5, 5)
            attention(1)
            pe.wait_ge(sel_done, 1)
            broadcast(0, 6)
            transpose_pair(2)
            broadcast(1, 10)
            mod_unit(6, 14)
            mod_unit(7, 15)
            attention(2)
            broadcast(2, 16)
            transpose_pair(3)
            broadcast(3, 20)
            gating(0)
            attention(3)
            gating(1)
            for b in range(2, NB):
                for t in range(PAIR):
                    ranks(PAIR * (b - 2) + t)
                gating(b)
            for n in range(4, NT):
                ranks(n)

            pe.wait_ge(logits_read, NT)
            t_.matmul(ps_m[0:E, 0, 0:P], before[:, NT, :], ones, start=True, stop=True
                      ).then_inc(total_done, 1)
            pe.wait_ge(over_ready, 1)
            t_.matmul(ps_m[:, 0, 0:E + 1], over[:], upper, start=True, stop=True)
            t_.matmul(ps_m[0:E, 0, 64:65], upper_inc, over[:, 0:1], start=True, stop=True
                      ).then_inc(base_done, 1)
            for r in range(K * NT):
                pe.wait_ge(row_hot_ready, r + 1)
                pe.wait_ge(col_hot_ready, 2 * r + 2)
                t_.matmul(ps_t[:, 0, 0:2 * NCOL], row_hot[:, r % 8, :], col_hot[:, r % 8, :],
                          start=(r == 0), stop=(r == K * NT - 1)).then_inc(table_done, 1)
            pe.wait_ge(owner_ready, 1)
            t_.matmul(ps_m[0:1, 0, 0:16], ones[0:E, 0:1], over_cmp[:], start=True, stop=True
                      ).then_inc(owner_done, 1)

            def transpose_rows(e0, u):
                pe.wait_ge(gathered[u % 4], e0 * 4 + 16 * (u // 4 + 1))
                for c in range(NC):
                    ins = t_.transpose(ps_t[:, u % 2, c * P:(c + 1) * P], g[:, u % 4, c * P:(c + 1) * P],
                                       ident)
                ins.then_inc(g_used, 1)

            pe.wait_ge(share_ready, 1)
            for n in range(NT):
                ins = t_.transpose(ps_t[0:E, 2 + n // 4, (n % 4) * P:(n % 4 + 1) * P], prod[:, n, :], ident)
                if n % 4 == 3:
                    ins.then_inc(share_t_done, 1)
            transpose_rows(0, 0)
            pe.wait_ge(share_t_read, 2)
            pe.wait_ge(bexp_landed, 16)
            for n in range(NT):
                if n >= 2:
                    pe.wait_ge(bias_scaled, n - 1)
                t_.matmul(ps_y[:, n % 2, :], share_t[:, n * P:(n + 1) * P], b_exp, start=True, stop=True
                          ).then_inc(bias_done, 1)
            pe.wait_ge(owner_ready, 2)

            def step(e0, u):
                pe.wait_ge(xt_lo_done, e0 + u + 1)
                transpose_rows(e0, u + 1)
                pe.wait_ge(lo_ready, e0 * 2 + 2 * (FIRST + u + 1))
                pe.wait_ge(expert_read, e0 + u + 1)
                k, m = u % 2, slice((u % 2) * P, (u % 2 + 1) * P)
                product(ps_m[:, k, :], lambda c: ht_hi[:, c, m], lambda c: ht_lo[:, c, m],
                        lambda c: w_hi[:, k, c, :], lambda c: w_lo[:, k, c, :]).then_inc(expert_done, 1)

            with pe.Fori(0, E // RING) as i:
                for u in range(RING):
                    step(i * RING, u)

            pe.wait_ge(xt_lo_done, E + 1)
            count = pe.value_load(over_count[0:1, 0:1], min_val=0, max_val=NOV)
            with pe.Fori(0, NOV) as q:
                with pe.If(count > q):
                    pe.wait_ge(ov_g, 16 * q + 16)
                    for c in range(NC):
                        ins = t_.transpose(ps_t[:, 0, c * P:(c + 1) * P], g[:, 3, c * P:(c + 1) * P], ident)
                    ins.then_inc(ov_t, 1)
                    pe.wait_ge(ov_lo, 2 * q + 2)
                    product(ps_m[:, 0, :], lambda c: ht_hi[:, c, 0:P], lambda c: ht_lo[:, c, 0:P],
                            lambda c: w_hi[:, 0, c, :], lambda c: w_lo[:, 0, c, :]).then_inc(ov_y, 1)
                with pe.Else():
                    pe.nop()
                pe.nop()


def _constants():
    import numpy as np
    c = np.zeros((P, C_ALL), np.float32)
    i = np.arange(P)
    c[:, C_ID:C_ID + P] = i[:, None] == i[None, :]
    c[:, C_TRI:C_TRI + P] = i[:, None] < i[None, :]
    c[:, C_ONE:C_ONE + P] = 1
    c[:, C_IOTA:C_IOTA + P] = i[None, :]
    c[0:E, C_UP:C_UP + E] = i[0:E, None] < i[None, 0:E]
    c[0:E, C_UP + E] = 1
    c[0:E, C_INC:C_INC + E] = i[0:E, None] <= i[None, 0:E]
    r = np.arange(K * NT)
    c[:, C_PID:C_PID + K * NT] = r[None, :] * P + i[:, None] + 1
    for b in range(NB):
        c[b, C_SEL + b * P:C_SEL + (b + 1) * P] = 1
    return c


def kernel(L0_attn_x, L0_attn_w1, L0_attn_w2, L0_attn_b2, L0_attn_sparse_mask, L0_ffn_gate_w,
           L0_ffn_expert_w, L0_ffn_expert_b, L0_c, L0_wmod):
    import numpy as np
    import concourse.bacc as bacc
    from concourse.bass_utils import run_bass_kernel_spmd

    def chunked(a):
        return np.ascontiguousarray(a.reshape(NC, P, -1).transpose(1, 0, 2).reshape(P, -1))

    a = {k: np.asarray(v) for k, v in dict(
        x=L0_attn_x, w1=L0_attn_w1, w2=L0_attn_w2, b2=L0_attn_b2, mask=L0_attn_sparse_mask,
        gate=L0_ffn_gate_w, wexp=L0_ffn_expert_w, bexp=L0_ffn_expert_b, c=L0_c, wmod=L0_wmod).items()}
    arrays = {
        "in_x": a["x"].reshape(T, D),
        "in_w1": a["w1"],
        "in_w2t": np.ascontiguousarray(a["w2"].T),
        "in_b2": a["b2"],
        "in_maskt": chunked(a["mask"].T),
        "in_gatet": chunked(a["gate"].T),
        "in_wexp": np.ascontiguousarray(
            a["wexp"].reshape(E, D, NC, P).transpose(0, 3, 2, 1).reshape(E, P, UNIT)),
        "in_bexp": a["bexp"],
        "in_ct": np.ascontiguousarray(a["c"].T).reshape(P, NC * NB),
        "in_wmod": a["wmod"],
        "in_consts": _constants(),
    }
    nc = bacc.Bacc("TRN2", target_bir_lowering=False, num_devices=1)
    args = [nc.dram_tensor(n, v.shape, mybir.dt.from_np(v.dtype), kind="ExternalInput").ap()
            for n, v in arrays.items()]
    out = nc.dram_tensor("out_0", (NB, PAIR * P, D), F32, kind="ExternalOutput").ap()
    adaln_moe(nc, *args, out)
    r = run_bass_kernel_spmd(nc, [arrays], core_ids=[0])
    return r.results[0]["out_0"]
```

```python
from contextlib import ExitStack

import concourse.bass as bass
from concourse import mybir

F32 = mybir.dt.float32
F32R = mybir.dt.float32r
I32 = mybir.dt.int32
U32 = mybir.dt.uint32
ALU = mybir.AluOpType
ACT = mybir.ActivationFunctionType
AX_X = mybir.AxisListType.X

P = 128
D = 512
NC = D // P
T = 1024
NT = T // P
NB = 4
PAIR = NT // NB
E = 32
K = 2
NOV = (K * T - 1) // P
NCOL = 48
RING = 8
UNIT = NC * D
FIRST = 8
SPLIT = 2
GA, SB, CB, GB = range(4)
ROW_SA, COL_SA, ROW_CA, COL_CA = range(4)
ROW = {GA: 4, SB: 5, CB: 6, GB: 19}
CAST = {GA: 7, SB: 11, CB: 15, GB: 20}
M_JOBS = 24
AHEAD = 6
EPS = 1e-5
EMPTY = 4096.0

C_ID, C_TRI, C_ONE, C_IOTA = 0, 128, 256, 384
C_UP, C_INC, C_PID, C_SEL = 512, 512 + E + 1, 512 + 2 * E + 1, 512 + 2 * E + 1 + K * NT
C_ALL = C_SEL + NB * P


def adaln_moe(nc, x, w1, w2t, b2, maskt, gatet, wexp, bexp, ct, wmod, consts, out):
    ctx = ExitStack()
    with ctx:
        def sb(name, shape, dt=F32):
            return ctx.enter_context(nc.sbuf_tensor(name, shape, dt))

        def psum(name, shape):
            return ctx.enter_context(nc.psum_tensor(name, shape, F32))

        def sem(name):
            return ctx.enter_context(nc.semaphore(name))

        h2_rows = nc.dram_tensor("h2_rows", [T, D], F32).ap()
        y_rows = nc.dram_tensor("y_rows", [K * T, D], F32).ap()

        raw = sb("raw", [P, RING, UNIT])
        w_hi = sb("w_hi", [P, 2, NC, D], F32R)
        w_lo = sb("w_lo", [P, 2, NC, D], F32R)
        attn_hi = sb("attn_hi", [P, NC, D], F32R)
        attn_lo = sb("attn_lo", [P, NC, D], F32R)
        ht_hi = sb("ht_hi", [P, NC, PAIR * P], F32R)
        ht_lo = sb("ht_lo", [P, NC, PAIR * P], F32R)
        xs = sb("xs", [P, NT, D])
        norm = sb("norm", [P, PAIR, D])
        act = sb("act", [P, PAIR, D])
        h2 = sb("h2", [P, PAIR, D])
        bc = sb("bc", [P, 4, NB, D])
        g = sb("g", [P, 4, D])
        cst = sb("cst", [P, C_SEL])
        b2_bc = sb("b2_bc", [P, D])
        gate = sb("gate", [P, NC, E])
        c_raw = sb("c_raw", [P, NC, NB])
        c_silu = sb("c_silu", [P, NC, NB])
        sel = sb("sel", [NB, NB, P], F32R)
        mod_hi = sb("mod_hi", [NB, D], F32R)
        mod_lo = sb("mod_lo", [NB, D], F32R)
        mod_col = sb("mod_col", [P, 2, NC, NB])
        stats = sb("stats", [P, NT, 6])
        mv = sb("mv", [P, NT, 2])
        rstd = sb("rstd", [P, NT])
        half = sb("half", [P, NT])
        mv2 = sb("mv2", [P, NT, 2])
        rstd2 = sb("rstd2", [P, NT])
        logit = sb("logit", [P, E])
        top = sb("top", [P, NT, 8])
        top_at = sb("top_at", [P, PAIR, 8], U32)
        top_e = sb("top_e", [P, K, NT])
        hot = sb("hot", [P, K, NT, E])
        before = sb("before", [P, NT + 1, E])
        prod = sb("prod", [P, NT, E])
        place = sb("place", [P, K, NT])
        weight = sb("weight", [P, K, NT])
        w_tmp = sb("w_tmp", [P, 3, NT])
        over_base = sb("over_base", [P, E + 1])
        over_end = sb("over_end", [E, 1])
        over_cmp = sb("over_cmp", [E, 16])
        over_expert = sb("over_expert", [1, 16], I32)
        over_count = sb("over_count", [1, 1], I32)
        slot_w = sb("slot_w", [P, NCOL])
        gather_at = sb("gather_at", [P, NCOL], U32)
        scatter_at = sb("scatter_at", [P, NCOL], U32)
        over_at = sb("over_at", [P, 2], U32)
        sel_raw = h2[0:NB, 0, :]
        mod_tmp = g[0:NB, 2:4, :]
        row_sa, row_ca = bc[0:NB, GB, 2, :], bc[0:NB, GB, 1, :]
        row_of = [bc[0:NB, n, 3, :] for n in range(4)]
        ring_g = [h[:, c, :].bitcast(F32) for h in (attn_hi, attn_lo) for c in range(NC)]
        over_i = act[0:E, 0, 0:2 * P].bitcast(I32).rearrange("p (a m) -> p a m", a=2)
        over = act[0:E, 0, 2 * P:3 * P]
        place_f = act[:, 0, 3 * P:3 * P + 6 * K * NT].rearrange("p (a k n) -> p a k n", a=6, k=K)
        slot_f = act[:, 1, 0:3 * NCOL].rearrange("p (a n) -> p a n", a=3)
        place_i = act[:, 1, 3 * NCOL:3 * NCOL + 4 * K * NT].bitcast(I32).rearrange(
            "p (a k n) -> p a k n", a=4, k=K)
        rank = act[:, 1, 256:256 + NT * E].rearrange("p (n e) -> p n e", n=NT)
        row_hot = bc[:, SB, :, :].rearrange("p b d -> p (b d)").rearrange("p (r m) -> p r m", m=P)
        col_hot = bc[:, CB, :, :].rearrange("p b d -> p (b d)").rearrange("p (v m) -> p v m", v=2)[
            :, :, 0:K * NT * NCOL].rearrange("p v (r m) -> p v r m", m=NCOL)
        col_one = g[:, 2:4, :].rearrange("p a d -> p (a d)")[:, 0:K * NT * NCOL].rearrange(
            "p (r m) -> p r m", m=NCOL)
        ranked = norm[:, 0, :].rearrange("p (k n e) -> p k n e", k=K, n=NT)
        bias_row = [norm[:, 0, :], norm[:, 1, :], h2[:, 0, :], h2[:, 1, :]]
        share_t = bc[0:E, 0, 0:2, :].rearrange("p a d -> p (a d)")
        b_exp = bc[0:E, 0, 2, :]

        ps_t = psum("ps_t", [P, 4, 512])
        ps_y = psum("ps_y", [P, 2, 512])
        ps_m = psum("ps_m", [P, 2, 512])

        ident = cst[:, C_ID:C_ID + P]
        tri = cst[:, C_TRI:C_TRI + P]
        ones = cst[:, C_ONE:C_ONE + P]
        iota = cst[:, C_IOTA:C_IOTA + P]
        upper = cst[0:E, C_UP:C_UP + E + 1]
        upper_inc = cst[0:E, C_INC:C_INC + E]
        pair_id = cst[:, C_PID:C_PID + K * NT].rearrange("p (k n) -> p k n", k=K)

        consts_landed = sem("consts_landed")
        params_landed = sem("params_landed")
        raw_landed = [sem(f"raw_landed{s}") for s in range(RING)]
        x_landed = [sem(f"x_landed{s}") for s in range(2)]
        mask_landed = sem("mask_landed")
        h2_written = [sem(f"h2_written{s}") for s in range(2)]
        bexp_landed = sem("bexp_landed")
        silu_done = sem("silu_done")
        sel_done = sem("sel_done")
        hi_ready = sem("hi_ready")
        lo_ready = sem("lo_ready")
        m_done = sem("m_done")
        m_read = sem("m_read")
        gains_ready = sem("gains_ready")
        mod_hi_done = sem("mod_hi_done")
        mod_lo_done = sem("mod_lo_done")
        col_ready = sem("col_ready")
        attn_done = sem("attn_done")
        attn_read = sem("attn_read")
        attn_hi_done = sem("attn_hi_done")
        attn_lo_done = sem("attn_lo_done")
        stats_done = sem("stats_done")
        half_done = sem("half_done")
        rstd_done = sem("rstd_done")
        norm_ready = sem("norm_ready")
        t_done = sem("t_done")
        ht_ready = sem("ht_ready")
        ht_hi_done = sem("ht_hi_done")
        ht_lo_done = sem("ht_lo_done")
        y_done = sem("y_done")
        y_read = sem("y_read")
        gelu_done = sem("gelu_done")
        x2_ready = sem("x2_ready")
        stats2_done = sem("stats2_done")
        rstd2_done = sem("rstd2_done")
        h2_ready = sem("h2_ready")
        t2_done = sem("t2_done")
        h2t_ready = sem("h2t_ready")
        logits_done = sem("logits_done")
        logits_read = sem("logits_read")
        picks_ready = sem("picks_ready")
        ranks_done = sem("ranks_done")
        total_done = sem("total_done")
        over_ready = sem("over_ready")
        base_done = sem("base_done")
        base_read = sem("base_read")
        owner_done = sem("owner_done")
        owner_ready = sem("owner_ready")
        exp_in = sem("exp_in")
        exp_done = sem("exp_done")
        weight_ready = sem("weight_ready")
        place_ready = sem("place_ready")
        row_hot_ready = sem("row_hot_ready")
        col_one_ready = sem("col_one_ready")
        col_hot_ready = [sem(f"col_hot_ready{v}") for v in range(2)]
        table_done = [sem(f"table_done{v}") for v in range(2)]
        weights_ready = sem("weights_ready")
        slots_ready = sem("slots_ready")
        share_ready = sem("share_ready")
        share_t_done = sem("share_t_done")
        share_t_read = sem("share_t_read")
        bias_done = sem("bias_done")
        bias_scaled = sem("bias_scaled")
        bias_added = sem("bias_added")
        gathered = [sem(f"gathered{s}") for s in range(8)]
        g_used = sem("g_used")
        xt_hi_done = sem("xt_hi_done")
        xt_lo_done = sem("xt_lo_done")
        expert_done = sem("expert_done")
        expert_read = sem("expert_read")
        scattered = [sem(f"scattered{s}") for s in range(4)]
        ov_w = sem("ov_w")
        ov_at = sem("ov_at")
        ov_g = sem("ov_g")
        ov_t = sem("ov_t")
        ov_hi = sem("ov_hi")
        ov_lo = sem("ov_lo")
        ov_y = sem("ov_y")
        ov_out = sem("ov_out")
        rows_left = sem("rows_left")
        ov_turn = sem("ov_turn")
        ov_done = sem("ov_done")
        rows_complete = sem("rows_complete")
        rows_landed = [sem(f"rows_landed{n}") for n in range(NT)]
        sum_ready = sem("sum_ready")
        out_ready = [sem(f"out_ready_{w}") for w in ("pool", "dve")]
        stored = sem("stored")
        dve_chain = sem("dve_chain")
        pool_chain = sem("pool_chain")

        def unit_source(j):
            if j >= 2:
                return wmod.rearrange("(p c) n -> p c n", c=NC)[:, :, (j - 2) * D:(j - 1) * D]
            return (w1, w2t)[j].rearrange("(p c) n -> p c n", c=NC)

        def slot3(s):
            return raw[:, s, :].rearrange("p (c n) -> p c n", c=NC)

        block = ctx.enter_context(nc.Block())

        @block.sync
        def _(sp):
            sp.dma_start(c_raw[:], ct.rearrange("p (c b) -> p c b", c=NC)).then_inc(consts_landed, 16)
            sp.dma_start(cst[:], consts[:, 0:C_SEL]).then_inc(consts_landed, 16)
            sp.dma_start(sel_raw, consts[0:NB, C_SEL:C_ALL]).then_inc(consts_landed, 16)

            def load_unit(j):
                sp.dma_start(slot3(j), unit_source(j)).then_inc(raw_landed[j], 16)

            load_unit(0)
            load_unit(1)
            sp.dma_start(g[:], maskt.rearrange("p (c n) -> p c n", c=NC)).then_inc(mask_landed, 16)
            x_v = x.rearrange("(n p) d -> p n d", p=P)
            for s in range(2):
                n = slice(s * NT // 2, (s + 1) * NT // 2)
                sp.dma_start(xs[:, n, :], x_v[:, n, :]).then_inc(x_landed[s], 16)
            load_unit(2)
            load_unit(3)
            sp.dma_start(b2_bc[:], b2.rearrange("(a n) -> a n", a=1).broadcast_to([P, D])
                         ).then_inc(params_landed, 16)
            sp.dma_start(gate[:], gatet.rearrange("p (c n) -> p c n", c=NC)).then_inc(params_landed, 16)
            for j in range(4, FIRST):
                load_unit(j)

            def load_expert(e, u):
                sp.dma_start(raw[:, u, :], wexp[bass.ds(e, 1), :, :].rearrange("a p n -> (a p) n")
                             ).then_inc(raw_landed[u], 16)

            def store_h2(n):
                sp.wait_ge(h2_ready, n + 1)
                sp.dma_start(h2_rows[n * P:(n + 1) * P, :], h2[:, n % 2, :]).then_inc(h2_written[n % 2], 16)

            for u in range(SPLIT):
                sp.wait_ge(lo_ready, 2 * u + 2)
                load_expert(u, u)
            for u, job in enumerate((ROW_SA, ROW_CA, ROW[GA], ROW[SB], ROW[CB]), SPLIT):
                sp.wait_ge(m_done, job + 1)
                load_expert(u, u)
            for n in range(NT // 2):
                store_h2(n)
            sp.wait_ge(m_done, ROW[GB] + 1)
            load_expert(RING - 1, RING - 1)
            for n in range(NT // 2, NT):
                store_h2(n)
            with sp.Fori(1, E // RING) as i:
                for u in range(RING):
                    sp.wait_ge(lo_ready, i * (2 * RING) + 2 * (SPLIT + u + 1 - RING))
                    load_expert(i * RING + u, u)

            sp.wait_ge(owner_ready, 2)
            count = sp.value_load(over_count[0:1, 0:1], min_val=0, max_val=NOV)
            sp.wait_ge(lo_ready, 2 * (SPLIT + E))
            with sp.If(count > 0):
                with sp.Fori(0, NOV) as q:
                    with sp.If(count > q):
                        owner = sp.value_load(over_expert[0:1, bass.ds(q, 1)], min_val=0, max_val=E - 1)
                        sp.wait_ge(ov_done, q + 1)
                        sp.dma_start(raw[:, 0, :], wexp[bass.ds(owner, 1), :, :].rearrange(
                            "a p n -> (a p) n")).then_inc(ov_w, 16)
                    with sp.Else():
                        sp.nop()
                    sp.nop()
                sp.nop()
            with sp.Else():
                sp.nop()
            sp.wait_ge(rows_complete, 1)
            y_v = y_rows.rearrange("(k n p) d -> n p k d", p=P, k=K)
            for n in range(NT):
                sp.dma_start(raw[:, n, 0:K * D].rearrange("p (k d) -> p k d", k=K), y_v[n]
                             ).then_inc(rows_landed[n], 16)
            out_v = out.rearrange("b (a p) d -> (b a) p d", p=P)
            for n in range(NT):
                sp.wait_ge(out_ready[n % 2], n // 2 + 1)
                sp.dma_start(out_v[n], xs[:, n, :]).then_inc(stored, 16)
            sp.wait_ge(stored, 16 * NT)

        @block.scalar
        def _(a):
            s = nc.scalar
            a.wait_ge(consts_landed, 3 * 16)
            s.activation(c_silu[:], c_raw[:], ACT.Silu).then_inc(silu_done, 1)
            s.copy(sel[:], sel_raw.rearrange("p (b m) -> p b m", b=NB)).then_inc(sel_done, 1)

            def split_hi(u, slot):
                for h in range(2):
                    c = slice(2 * h, 2 * h + 2)
                    s.copy(w_hi[:, u % 2, c, :], slot3(slot)[:, c, :]).then_inc(hi_ready, 1)

            def read_m(job, dst, src):
                a.wait_ge(m_done, job + 1)
                s.copy(dst, src).then_inc(m_read, 1)

            def read_row(job, dst):
                read_m(job, dst, ps_m[0:NB, job % 2, :])

            def read_col(job, n):
                read_m(job, mod_col[:, n, :, :].rearrange("p c b -> p (c b)"), ps_m[:, job % 2, 0:NC * NB])

            def section_hi(n):
                if n in (GA, GB):
                    a.wait_ge(gains_ready, 1 + (n == GB))
                else:
                    a.wait_ge(m_read, ROW[n] + 1)
                if n != GA:
                    a.wait_ge(m_done, CAST[n - 1] + NB)
                s.copy(mod_hi[:], row_of[n]).then_inc(mod_hi_done, 1)

            def read_cast(n, batches=range(NB)):
                for b in batches:
                    job = CAST[n] + b
                    read_m(job, bc[:, n, b, :], ps_m[:, job % 2, :])

            def modulate(n):
                a.wait_ge(t_done, n + 1)
                if n == 0:
                    a.wait_ge(col_ready, 1)
                b = n // PAIR
                nt = norm[:, n % 2, :].rearrange("p (c m) -> p c m", c=NC)
                for c in range(NC):
                    s.activation(nt[:, c, :], ps_t[:, n % 2, c * P:(c + 1) * P], ACT.Identity,
                                 bias=mod_col[:, 0, c, b:b + 1], scale=mod_col[:, 1, c, b:b + 1]
                                 ).then_inc(ht_ready, 1)
                if n >= 2:
                    a.wait_ge(y_done, n - 1)
                a.wait_ge(ht_ready, NC * (n + 1))
                s.copy(ht_hi[:, :, (n % 2) * P:(n % 2 + 1) * P], nt).then_inc(ht_hi_done, 1)

            def gelu(n):
                a.wait_ge(y_read, n + 1)
                s.activation(act[:, n % 2, :], act[:, n % 2, :], ACT.Gelu).then_inc(gelu_done, 1)

            def copy_h2t(n):
                a.wait_ge(t2_done, n + 1)
                if n >= 2:
                    a.wait_ge(logits_done, n - 1)
                s.copy(g[:, n % 2, :], ps_t[:, 2 + n % 2, :]).then_inc(h2t_ready, 1)

            def expert_hi(e0, u):
                if isinstance(e0, int) and e0 + u < 2:
                    a.wait_ge(attn_done, NC)
                else:
                    a.wait_ge(expert_done, e0 + u)
                a.wait_ge(raw_landed[u % RING], e0 * 2 + 16 * (2 + u // RING))
                split_hi(u, u % RING)

            for u in range(SPLIT):
                a.wait_ge(raw_landed[u], 16)
                split_hi(u, u)
            for c in range(NC):
                a.wait_ge(attn_read, c + 1)
                s.copy(attn_hi[:, c, :], h2[:, c % 2, :]).then_inc(attn_hi_done, 1)
            read_row(ROW_SA, row_sa)
            read_col(COL_SA, 0)
            read_row(ROW_CA, row_ca)
            read_col(COL_CA, 1)
            modulate(0)
            modulate(1)
            read_row(ROW[GA], row_of[GA])
            modulate(2)
            gelu(0)
            read_row(ROW[SB], row_of[SB])
            section_hi(GA)
            read_row(ROW[CB], row_of[CB])
            modulate(3)
            gelu(1)
            read_cast(GA)
            section_hi(SB)
            modulate(4)
            gelu(2)
            read_cast(SB)
            section_hi(CB)
            modulate(5)
            gelu(3)
            read_cast(CB)
            modulate(6)
            gelu(4)
            copy_h2t(0)
            modulate(7)
            gelu(5)
            copy_h2t(1)
            expert_hi(0, 0)
            gelu(6)
            copy_h2t(2)
            gelu(7)
            copy_h2t(3)
            read_row(ROW[GB], row_of[GB])
            copy_h2t(4)
            section_hi(GB)
            copy_h2t(5)
            read_cast(GB)
            copy_h2t(6)
            a.wait_ge(x2_ready, NT)
            a.dma_start(b_exp, bexp).then_inc(bexp_landed, 16)
            copy_h2t(7)
            expert_hi(0, 1)
            a.wait_ge(exp_in, 1)
            s.activation(w_tmp[:, 1, :], w_tmp[:, 0, :], ACT.Exp).then_inc(exp_done, 1)

            def rows_hi(e0, u):
                a.wait_ge(g_used, e0 + u + 1)
                a.wait_ge(expert_done, e0 + u)
                k = u % 2
                s.copy(ht_hi[:, :, k * P:(k + 1) * P], ps_t[:, k, :].rearrange("p (c m) -> p c m", c=NC)
                       ).then_inc(xt_hi_done, 1)

            def rows_out(e0, u):
                a.wait_ge(expert_done, e0 + u + 2)
                a.wait_ge(rows_left, e0 + u + 1)
                s.activation(g[:, u % 4, :], ps_m[:, u % 2, :], ACT.Copy,
                             scale=slot_w[:, bass.ds(e0 + u, 1)]).then_inc(expert_read, 1)

            def step(e0, u, last=False):
                rows_hi(e0, u + 1)
                rows_out(e0, u)
                if not (last and u >= RING - 2):
                    expert_hi(e0, u + 2)

            a.wait_ge(g_used, 1)
            s.copy(ht_hi[:, :, 0:P], ps_t[:, 0, :].rearrange("p (c m) -> p c m", c=NC)
                   ).then_inc(xt_hi_done, 1)
            for h in range(2):
                a.wait_ge(share_t_done, h + 1)
                s.copy(share_t[:, h * 512:(h + 1) * 512], ps_t[0:E, 2 + h, :]).then_inc(share_t_read, 1)
            a.wait_ge(weights_ready, 1)
            with a.Fori(0, E // RING - 1) as i:
                for u in range(RING):
                    step(i * RING, u)
            for u in range(RING):
                step(E - RING, u, last=True)

            count = a.value_load(over_count[0:1, 0:1], min_val=0, max_val=NOV)
            with a.If(count > 0):
                with a.Fori(0, NOV) as q:
                    with a.If(count > q):
                        a.wait_ge(ov_w, 16 * q + 16)
                        s.copy(w_hi[:, 0, :, :], slot3(0)).then_inc(ov_hi, 1)
                        a.wait_ge(ov_t, q + 1)
                        s.copy(ht_hi[:, :, 0:P], ps_t[:, 0, :].rearrange("p (c m) -> p c m", c=NC)
                               ).then_inc(ov_hi, 1)
                        a.wait_ge(ov_y, q + 1)
                        s.activation(act[:, 0, :], ps_m[:, 0, :], ACT.Copy, scale=slot_w[:, bass.ds(q + E, 1)]
                                     ).then_inc(ov_out, 1)
                    with a.Else():
                        a.nop()
                    a.nop()
                a.nop()
            with a.Else():
                a.nop()

        @block.vector
        def _(v):
            d = nc.vector
            linked = [0]

            def link(ins):
                linked[0] += 1
                ins.then_inc(dve_chain, 1)
                v.wait_ge(dve_chain, linked[0])

            def split_lo(j, slot, need):
                for h in range(2):
                    c = slice(2 * h, 2 * h + 2)
                    v.wait_ge(hi_ready, need + h + 1)
                    d.tensor_tensor(w_lo[:, j % 2, c, :], slot3(slot)[:, c, :],
                                    w_hi[:, j % 2, c, :].bitcast(F32), ALU.subtract).then_inc(lo_ready, 1)

            def expert_lo(e0, u):
                split_lo(u, u % RING, e0 * 2 + 2 * (SPLIT + u))

            def norm_stats(m, n, done):
                link(d.bn_stats(stats[:, n, :], xs[:, n, :]))
                d.bn_aggr(m[:, n, :], stats[:, n, :]).then_inc(done, 1)

            def norm_rows(n):
                if n >= 2:
                    v.wait_ge(ht_lo_done, n - 1)
                d.tensor_scalar(norm[:, n % 2, :], xs[:, n, :], mv[:, n, 0:1], rstd[:, n:n + 1],
                                ALU.subtract, ALU.mult).then_inc(norm_ready, 1)

            def mask_attn(c):
                v.wait_ge(attn_done, c + 1)
                if c >= 2:
                    v.wait_ge(attn_lo_done, c - 1)
                d.tensor_tensor(h2[:, c % 2, :], ps_t[:, c, :], g[:, c, :], ALU.mult).then_inc(attn_read, 1)

            def attn_lo_part(c):
                v.wait_ge(attn_hi_done, c + 1)
                d.tensor_tensor(attn_lo[:, c, :], h2[:, c % 2, :], attn_hi[:, c, :].bitcast(F32),
                                ALU.subtract).then_inc(attn_lo_done, 1)

            def ht_lo_part(n):
                v.wait_ge(ht_hi_done, n + 1)
                m = slice((n % 2) * P, (n % 2 + 1) * P)
                d.tensor_tensor(ht_lo[:, :, m], norm[:, n % 2, :].rearrange("p (c m) -> p c m", c=NC),
                                ht_hi[:, :, m].bitcast(F32), ALU.subtract).then_inc(ht_lo_done, 1)

            def add_b2(n):
                v.wait_ge(y_done, n + 1)
                if n >= 2:
                    v.wait_ge(x2_ready, n - 1)
                d.tensor_tensor(act[:, n % 2, :], ps_y[:, n % 2, :], b2_bc[:], ALU.add).then_inc(y_read, 1)

            def bound_gain(n, turn):
                v.wait_ge(m_read, ROW[n] + 1)
                row = row_of[n]
                link(d.tensor_scalar(mod_tmp[:, 0, :], row, 0.0, 2.0, ALU.is_ge, ALU.mult))
                link(d.tensor_scalar(mod_tmp[:, 0, :], mod_tmp[:, 0, :], -1.0, None, ALU.add))
                link(d.scalar_tensor_tensor(out=mod_tmp[:, 1, :], in0=row, scalar=-1.0, in1=row,
                                            op0=ALU.mult, op1=ALU.max))
                d.scalar_tensor_tensor(out=row, in0=mod_tmp[:, 1, :], scalar=0.25, in1=mod_tmp[:, 0, :],
                                       op0=ALU.max, op1=ALU.mult).then_inc(gains_ready, 1)
                v.wait_ge(gains_ready, turn + 1)

            def section_lo(n):
                v.wait_ge(mod_hi_done, n + 1)
                d.tensor_tensor(mod_lo[:], row_of[n], mod_hi[:].bitcast(F32), ALU.subtract
                                ).then_inc(mod_lo_done, 1)

            def second_stats(n):
                v.wait_ge(x2_ready, n + 1)
                norm_stats(mv2, n, stats2_done)

            def scale_rows(n):
                v.wait_ge(rstd2_done, n + 1)
                b, row = n // PAIR, h2[:, n % 2, :]
                if n < 2:
                    v.wait_ge(attn_lo_done, NC)
                    v.wait_ge(m_read, CAST[CB] + NB)
                else:
                    v.wait_ge(t2_done, n - 1)
                    v.wait_ge(h2_written[n % 2], 16 * (n // 2))
                link(d.tensor_scalar(row, xs[:, n, :], mv2[:, n, 0:1], rstd2[:, n:n + 1],
                                     ALU.subtract, ALU.mult))
                link(d.scalar_tensor_tensor(out=row, in0=bc[:, CB, b, :], scalar=1.0, in1=row,
                                            op0=ALU.add, op1=ALU.mult))
                d.tensor_tensor(row, row, bc[:, SB, b, :], ALU.add).then_inc(h2_ready, 1)

            def pick(n):
                v.wait_ge(logits_done, n + 1)
                link(d.max(top[:, n, :], ps_t[:, 2 + n % 2, 0:E]))
                d.max_index(top_at[:, n % 2, :], top[:, n, :], ps_t[:, 2 + n % 2, 0:E]).then_inc(logits_read, 1)

            def pick_hot(b):
                n = slice(PAIR * b, PAIR * (b + 1))
                v.wait_ge(logits_read, PAIR * (b + 1))
                link(d.tensor_copy(top_e[:, :, n].rearrange("p k n -> p n k"), top_at[:, :, 0:K]))
                link(d.tensor_tensor(hot[:, :, n, :],
                                     iota[:, 0:E].unsqueeze(1).unsqueeze(1).broadcast_to([P, K, PAIR, E]),
                                     top_e[:, :, n].unsqueeze(3).broadcast_to([P, K, PAIR, E]), ALU.is_equal))
                link(d.tensor_tensor(prod[:, n, :], hot[:, 0, n, :], hot[:, 1, n, :], ALU.add))
                for m in range(PAIR * b, PAIR * (b + 1)):
                    d.tensor_tensor(before[:, m + 1, :], before[:, m, :], prod[:, m, :], ALU.add
                                    ).then_inc(picks_ready, 1)
                    v.wait_ge(picks_ready, m + 1)

            link(d.memset(before[:, 0, :], 0.0))
            split_lo(0, 0, 0)
            split_lo(1, 1, 2)
            for n in range(NT):
                if n % (NT // 2) == 0:
                    v.wait_ge(x_landed[n // (NT // 2)], 16)
                norm_stats(mv, n, stats_done)
            v.wait_ge(rstd_done, 1)
            norm_rows(0)
            norm_rows(1)
            v.wait_ge(mask_landed, 16)
            v.wait_ge(sel_done, 1)
            mask_attn(0)
            mask_attn(1)
            attn_lo_part(0)
            mask_attn(2)
            attn_lo_part(1)
            mask_attn(3)
            attn_lo_part(2)
            attn_lo_part(3)
            v.wait_ge(m_read, COL_CA + 1)
            d.tensor_scalar(mod_col[:, 1, :, :], mod_col[:, 1, :, :], 1.0, None, ALU.add
                            ).then_inc(col_ready, 1)
            ht_lo_part(0)
            ht_lo_part(1)
            v.wait_ge(rstd_done, 2)
            norm_rows(2)
            norm_rows(3)
            bound_gain(GA, 0)
            v.wait_ge(params_landed, 2 * 16)
            add_b2(0)
            ht_lo_part(2)
            norm_rows(4)
            section_lo(GA)
            add_b2(1)
            ht_lo_part(3)
            norm_rows(5)
            add_b2(2)
            section_lo(SB)
            ht_lo_part(4)
            norm_rows(6)
            second_stats(0)
            add_b2(3)
            section_lo(CB)
            second_stats(1)
            ht_lo_part(5)
            norm_rows(7)
            add_b2(4)
            second_stats(2)
            scale_rows(0)
            ht_lo_part(6)
            add_b2(5)
            scale_rows(1)
            second_stats(3)
            ht_lo_part(7)
            pick(0)
            scale_rows(2)
            add_b2(6)
            second_stats(4)
            pick(1)
            scale_rows(3)
            add_b2(7)
            pick_hot(0)
            second_stats(5)
            pick(2)
            scale_rows(4)
            bound_gain(GB, 1)
            second_stats(6)
            pick(3)
            scale_rows(5)
            pick_hot(1)
            section_lo(GB)
            second_stats(7)
            pick(4)
            scale_rows(6)
            pick(5)
            scale_rows(7)
            pick_hot(2)
            expert_lo(0, 0)
            pick(6)
            pick(7)
            pick_hot(3)

            d.tensor_tensor(w_tmp[:, 0, :], top[:, :, 1], top[:, :, 0], ALU.subtract).then_inc(exp_in, 1)
            v.wait_ge(total_done, 1)
            link(d.tensor_scalar(over_i[:, 0, :], ps_m[0:E, 0, 0:P], float(P - 1), None, ALU.add))
            link(d.tensor_scalar(over_i[:, 1, :], over_i[:, 0, :], 7, None, ALU.arith_shift_right))
            d.tensor_scalar(over[:], over_i[:, 1, :], -1.0, 0.0, ALU.add, ALU.max).then_inc(over_ready, 1)
            v.wait_ge(exp_done, 1)
            link(d.tensor_scalar(w_tmp[:, 2, :], w_tmp[:, 1, :], 1.0, None, ALU.add))
            link(d.reciprocal(weight[:, 0, :], w_tmp[:, 2, :]))
            d.tensor_tensor(weight[:, 1, :], w_tmp[:, 1, :], weight[:, 0, :], ALU.mult
                            ).then_inc(weight_ready, 1)
            v.wait_ge(base_done, 1)
            d.tensor_copy(over_base[:], ps_m[:, 0, 0:E + 1]).then_inc(base_read, 1)
            d.tensor_copy(over_end[:], ps_m[0:E, 0, 64:65]).then_inc(base_read, 1)
            v.wait_ge(base_read, 2)
            v.wait_ge(ranks_done, NT)
            base = over_base[:, 0:E].unsqueeze(1).broadcast_to([P, NT, E])
            link(d.scalar_tensor_tensor(out=rank[:], in0=base, scalar=float(T),
                                        in1=ps_m[:, 1, 0:NT * E].rearrange("p (n e) -> p n e", n=NT),
                                        op0=ALU.mult, op1=ALU.add))
            rank_k = rank[:].unsqueeze(1).broadcast_to([P, K, NT, E])
            link(d.tensor_tensor(ranked[:], rank_k, hot[:], ALU.mult))
            link(d.tensor_reduce(place[:], ranked[:], AX_X, ALU.add))
            BOTH, RANK, OVER, LANE = range(4)
            link(d.tensor_copy(place_i[:, BOTH], place[:]))
            d.tensor_scalar(place_i[:, RANK], place_i[:, BOTH], T - 1, 7, ALU.bitwise_and,
                            ALU.arith_shift_right)
            d.tensor_scalar(place_i[:, OVER], place_i[:, BOTH], 10, None, ALU.arith_shift_right)
            link(d.tensor_scalar(place_i[:, LANE], place_i[:, BOTH], P - 1, None, ALU.bitwise_and))
            f_chunk, f_over, f_row, f_is, f_col, f_sum = (place_f[:, i] for i in range(6))
            d.tensor_copy(f_chunk, place_i[:, RANK])
            d.tensor_copy(f_over, place_i[:, OVER])
            link(d.tensor_copy(f_row, place_i[:, LANE]))
            link(d.tensor_scalar(f_is, f_chunk, 1.0, None, ALU.is_ge))
            link(d.scalar_tensor_tensor(out=f_sum, in0=f_chunk, scalar=float(E - 1), in1=f_over,
                                        op0=ALU.add, op1=ALU.add))
            link(d.tensor_tensor(f_sum, f_sum, top_e[:], ALU.subtract))
            link(d.tensor_tensor(f_sum, f_sum, f_is, ALU.mult))
            d.tensor_tensor(f_col, f_sum, top_e[:], ALU.add).then_inc(place_ready, 1)
            v.wait_ge(place_ready, 1)
            d.tensor_tensor(col_one[:], iota[:, 0:NCOL].unsqueeze(1).broadcast_to([P, K * NT, NCOL]),
                            place_f[:, 4].rearrange("p k n -> p (k n)").unsqueeze(2).broadcast_to(
                                [P, K * NT, NCOL]), ALU.is_equal).then_inc(col_one_ready, 1)
            for k in range(K):
                d.tensor_tensor(row_hot[:, k * NT:(k + 1) * NT, :],
                                iota.unsqueeze(1).broadcast_to([P, NT, P]),
                                place_f[:, 2, k, :].unsqueeze(2).broadcast_to([P, NT, P]), ALU.is_equal
                                ).then_inc(row_hot_ready, 1)
            v.wait_ge(table_done[0], 1)
            link(d.tensor_scalar(slot_f[:, 0, :], ps_t[:, 0, 0:NCOL], 0.0, EMPTY, ALU.is_equal, ALU.mult))
            link(d.scalar_tensor_tensor(out=slot_f[:, 1, :], in0=ps_t[:, 0, 0:NCOL], scalar=-1.0,
                                        in1=slot_f[:, 0, :], op0=ALU.add, op1=ALU.add))
            link(d.tensor_scalar(slot_f[:, 2, :], slot_f[:, 1, :], float(T), -float(T), ALU.is_ge,
                                 ALU.mult))
            d.tensor_tensor(gather_at[:], slot_f[:, 1, :], slot_f[:, 2, :], ALU.add).then_inc(slots_ready, 1)
            d.tensor_copy(scatter_at[:], slot_f[:, 1, :]).then_inc(slots_ready, 1)
            v.wait_ge(table_done[1], 1)
            d.tensor_copy(slot_w[:], ps_t[:, 1, 0:NCOL]).then_inc(weights_ready, 1)
            link(d.tensor_scalar(over_cmp[:], iota[0:E, 0:16], over_end[:, 0:1], None, ALU.is_ge))
            d.tensor_copy(over_count[:], over_base[0:1, E:E + 1]).then_inc(owner_ready, 1)
            expert_lo(0, 1)
            v.wait_ge(owner_done, 1)
            d.tensor_scalar(over_expert[:], ps_y[0:1, 0, 0:16], float(E - 1), None, ALU.min
                            ).then_inc(owner_ready, 1)

            def rows_lo(e0, u):
                v.wait_ge(xt_hi_done, e0 + u + 1)
                k = u % 2
                d.tensor_tensor(ht_lo[:, :, k * P:(k + 1) * P],
                                ps_t[:, k, :].rearrange("p (c m) -> p c m", c=NC),
                                ht_hi[:, :, k * P:(k + 1) * P].bitcast(F32), ALU.subtract
                                ).then_inc(xt_lo_done, 1)

            rows_lo(0, 0)
            for n in range(NT):
                v.wait_ge(bias_done, n + 1)
                if n == 0:
                    v.wait_ge(h2_written[0], 16 * (NT // 2))
                    v.wait_ge(h2_written[1], 16 * (NT // 2))
                if n >= 4:
                    v.wait_ge(bias_added, n - 3)
                d.tensor_tensor(bias_row[n % 4], ps_y[:, n % 2, :], bc[:, GB, n // PAIR, :], ALU.mult
                                ).then_inc(bias_scaled, 1)

            def step(e0, u, last=False):
                rows_lo(e0, u + 1)
                if not (last and u >= RING - 2):
                    expert_lo(e0, u + 2)

            with v.Fori(0, E // RING - 1) as i:
                for u in range(RING):
                    step(i * RING, u)
            for u in range(RING):
                step(E - RING, u, last=True)

            count = v.value_load(over_count[0:1, 0:1], min_val=0, max_val=NOV)
            with v.If(count > 0):
                with v.Fori(0, NOV) as q:
                    with v.If(count > q):
                        v.wait_ge(ov_hi, 2 * q + 1)
                        d.tensor_tensor(w_lo[:, 0, :, :], slot3(0), w_hi[:, 0, :, :].bitcast(F32),
                                        ALU.subtract).then_inc(ov_lo, 1)
                        v.wait_ge(ov_hi, 2 * q + 2)
                        d.tensor_tensor(ht_lo[:, :, 0:P], ps_t[:, 0, :].rearrange("p (c m) -> p c m", c=NC),
                                        ht_hi[:, :, 0:P].bitcast(F32), ALU.subtract).then_inc(ov_lo, 1)
                    with v.Else():
                        v.nop()
                    v.nop()
                v.nop()
            with v.Else():
                v.nop()

            v.wait_ge(bias_added, NT)
            for n in range(NT):
                v.wait_ge(rows_landed[n], 16)
                a_, b_ = raw[:, n, 0:D], raw[:, n, D:2 * D]
                link(d.tensor_tensor(a_, a_, b_, ALU.add))
                if n % 2 == 0:
                    d.tensor_tensor(a_, a_, bc[:, GB, n // PAIR, :], ALU.mult).then_inc(sum_ready, 1)
                else:
                    link(d.tensor_tensor(a_, a_, bc[:, GB, n // PAIR, :], ALU.mult))
                    d.tensor_tensor(xs[:, n, :], xs[:, n, :], a_, ALU.add).then_inc(out_ready[1], 1)

        @block.gpsimd
        def _(p):
            q7 = nc.gpsimd
            p.sem_inc(expert_done, 1)
            p.sem_inc(expert_read, 2)
            p.sem_inc(rows_left, 4)
            p.sem_inc(ov_done, 1)
            q7.memset(half[:], -0.5).then_inc(half_done, 1)
            p.wait_ge(half_done, 1)

            chained = [0]

            def link(ins):
                chained[0] += 1
                ins.then_inc(pool_chain, 1)
                p.wait_ge(pool_chain, chained[0])

            def power(m, out_, n0, n1, done):
                link(q7.tensor_scalar(out_[:, n0:n1], m[:, n0:n1, 1], EPS, None, ALU.add))
                q7.tensor_tensor(out_[:, n0:n1], out_[:, n0:n1], half[:, n0:n1], ALU.pow).then_inc(done, 1)

            p.wait_ge(stats_done, NT // 2)
            power(mv, rstd, 0, NT // 2, rstd_done)
            p.wait_ge(stats_done, NT)
            power(mv, rstd, NT // 2, NT, rstd_done)

            def add_attn(n):
                p.wait_ge(gelu_done, n + 1)
                if n == 0:
                    p.wait_ge(m_read, CAST[GA] + NB)
                row = act[:, n % 2, :]
                link(q7.tensor_tensor(row, row, bc[:, GA, n // PAIR, :], ALU.mult))
                q7.tensor_tensor(xs[:, n, :], xs[:, n, :], row, ALU.add).then_inc(x2_ready, 1)

            def second_rstd(n):
                p.wait_ge(stats2_done, n + 1)
                power(mv2, rstd2, n, n + 1, rstd2_done)

            add_attn(0)
            for n in range(1, NT):
                add_attn(n)
                second_rstd(n - 1)
            second_rstd(NT - 1)

            p.wait_ge(col_one_ready, 1)
            for v_, val in enumerate((pair_id, weight[:])):
                if v_ == 1:
                    p.wait_ge(weight_ready, 1)
                q7.tensor_tensor(col_hot[:, v_], col_one[:],
                                 val.rearrange("p k n -> p (k n)").unsqueeze(2).broadcast_to(
                                     [P, K * NT, NCOL]), ALU.mult).then_inc(col_hot_ready[v_], 1)

            def gather(at, s, done):
                q7.indirect_dma_start(ring_g[s], None, h2_rows, bass.IndirectOffsetOnAxis(ap=at, axis=0),
                                      bounds_check=T - 1, oob_is_err=False).then_inc(done, 16)

            def scatter(at, rows, done):
                q7.indirect_dma_start(y_rows, bass.IndirectOffsetOnAxis(ap=at, axis=0), rows, None,
                                      bounds_check=K * T - 1, oob_is_err=False).then_inc(done, 16)

            p.wait_ge(h2_written[0], 16 * (NT // 2))
            p.wait_ge(h2_written[1], 16 * (NT // 2))
            p.wait_ge(y_done, NT)
            p.wait_ge(slots_ready, 2)
            for e in range(AHEAD):
                gather(gather_at[:, e:e + 1], e, gathered[e])

            w0 = weight[:, 0, :].unsqueeze(2).broadcast_to([P, NT, E])
            w1_ = weight[:, 1, :].unsqueeze(2).broadcast_to([P, NT, E])
            link(q7.tensor_tensor(prod[:], hot[:, 0], w0, ALU.mult))
            link(q7.tensor_tensor(rank[:], hot[:, 1], w1_, ALU.mult))
            q7.tensor_tensor(prod[:], prod[:], rank[:], ALU.add).then_inc(share_ready, 1)
            for n in range(NT):
                p.wait_ge(bias_scaled, n + 1)
                q7.tensor_tensor(xs[:, n, :], xs[:, n, :], bias_row[n % 4], ALU.add).then_inc(bias_added, 1)

            for e in range(E):
                ahead = e + AHEAD
                if ahead <= E:
                    if ahead >= 8:
                        p.wait_ge(g_used, ahead - 7)
                    gather(gather_at[:, ahead:ahead + 1], ahead % 8, gathered[ahead % 8])
                if e >= 3:
                    p.wait_ge(scattered[(e - 3) % 4], 16 * ((e - 3) // 4 + 1))
                    p.sem_inc(rows_left, 1)
                p.wait_ge(expert_read, e + 3)
                scatter(scatter_at[:, e:e + 1], g[:, e % 4, :], scattered[e % 4])

            p.wait_ge(owner_ready, 2)
            count = p.value_load(over_count[0:1, 0:1], min_val=0, max_val=NOV)
            for s in range(4):
                p.wait_ge(scattered[s], 16 * (E // 4))
            for s in range(8):
                p.wait_ge(gathered[s], 16 * (E // 8 + (s == 0)))
            with p.If(count > 0):
                with p.Fori(0, NOV) as q:
                    with p.If(count > q):
                        q7.tensor_copy(over_at[:, 0:1], gather_at[:, bass.ds(q + E, 1)]).then_inc(ov_at, 1)
                        q7.tensor_copy(over_at[:, 1:2], scatter_at[:, bass.ds(q + E, 1)]).then_inc(ov_at, 1)
                        p.wait_ge(ov_at, 2 * q + 2)
                        p.sem_inc(ov_turn, 1)
                        gather(over_at[:, 0:1], 1, ov_g)
                        p.wait_ge(ov_out, q + 1)
                        p.sem_inc(ov_turn, 1)
                        scatter(over_at[:, 1:2], act[:, 0, :], scattered[0])
                        p.wait_ge(scattered[0], 16 * q + 16 * (E // 4 + 1))
                        p.sem_inc(ov_done, 1)
                    with p.Else():
                        p.nop()
                    p.nop()
                p.nop()
            with p.Else():
                p.nop()
            p.sem_inc(rows_complete, 1)

            for n in range(0, NT, 2):
                p.wait_ge(sum_ready, n // 2 + 1)
                q7.tensor_tensor(xs[:, n, :], xs[:, n, :], raw[:, n, 0:D], ALU.add).then_inc(out_ready[0], 1)

        @block.tensor
        def _(pe):
            t_ = nc.tensor

            def product(out_, l_hi, l_lo, r_hi, r_lo):
                for c in range(NC):
                    t_.matmul(out_, l_hi(c), r_hi(c), start=(c == 0), stop=False)
                    t_.matmul(out_, l_hi(c), r_lo(c), start=False, stop=False)
                    ins = t_.matmul(out_, l_lo(c), r_hi(c), start=False, stop=(c == NC - 1))
                return ins

            def mod_row(slot, job):
                pe.wait_ge(raw_landed[slot], 16)
                if job >= 2:
                    pe.wait_ge(m_read, job - 1)
                for c in range(NC):
                    ins = t_.matmul(ps_m[0:NB, job % 2, :], c_silu[:, c, :], slot3(slot)[:, c, :],
                                    start=(c == 0), stop=(c == NC - 1))
                ins.then_inc(m_done, 1)

            def mod_columns(row, job):
                pe.wait_ge(m_read, job)
                for c in range(NC):
                    ins = t_.transpose(ps_m[:, job % 2, c * NB:(c + 1) * NB], row[:, c * P:(c + 1) * P],
                                       ident[0:NB, 0:NB])
                ins.then_inc(m_done, 1)

            def broadcast(n, turn):
                pe.wait_ge(mod_lo_done, turn + 1)
                for b in range(NB):
                    job = CAST[n] + b
                    pe.wait_ge(m_read, job - 1)
                    t_.matmul(ps_m[:, job % 2, :], sel[:, b, :], mod_hi[:], start=True, stop=False)
                    t_.matmul(ps_m[:, job % 2, :], sel[:, b, :], mod_lo[:], start=False, stop=True
                              ).then_inc(m_done, 1)

            def transposes(n):
                pe.wait_ge(norm_ready, n + 1)
                if n < 2:
                    pe.wait_ge(attn_read, n + 1)
                else:
                    pe.wait_ge(ht_ready, NC * (n - 1))
                for c in range(NC):
                    ins = t_.transpose(ps_t[:, n % 2, c * P:(c + 1) * P], norm[:, n % 2, c * P:(c + 1) * P],
                                       ident)
                ins.then_inc(t_done, 1)

            def attention(n):
                pe.wait_ge(ht_lo_done, n + 1)
                if n == 0:
                    pe.wait_ge(attn_lo_done, NC)
                if n >= 2:
                    pe.wait_ge(y_read, n - 1)
                m = slice((n % 2) * P, (n % 2 + 1) * P)
                product(ps_y[:, n % 2, :], lambda c: ht_hi[:, c, m], lambda c: ht_lo[:, c, m],
                        lambda c: attn_hi[:, c, :], lambda c: attn_lo[:, c, :]).then_inc(y_done, 1)

            def transposes2(n):
                pe.wait_ge(h2_ready, n + 1)
                if n < 2:
                    pe.wait_ge(attn_read, NC)
                else:
                    pe.wait_ge(logits_read, n - 1)
                for c in range(NC):
                    ins = t_.transpose(ps_t[:, 2 + n % 2, c * P:(c + 1) * P], h2[:, n % 2, c * P:(c + 1) * P],
                                       ident)
                ins.then_inc(t2_done, 1)

            def logits(n):
                pe.wait_ge(h2t_ready, n + 1)
                for c in range(NC):
                    ins = t_.matmul(ps_t[:, 2 + n % 2, 0:E], g[:, n % 2, c * P:(c + 1) * P], gate[:, c, :],
                                    start=(c == 0), stop=(c == NC - 1))
                ins.then_inc(logits_done, 1)

            def ranks(n):
                pe.wait_ge(picks_ready, n + 1)
                o = ps_m[:, 1, n * E:(n + 1) * E]
                t_.matmul(o, tri, prod[:, n, :], start=True, stop=False)
                t_.matmul(o, ones, before[:, n, :], start=False, stop=True).then_inc(ranks_done, 1)

            def table(val, bank):
                for r in range(K * NT):
                    ins = t_.matmul(ps_t[:, bank, 0:NCOL], row_hot[:, r, :], col_hot[:, val, r, :],
                                    start=(r == 0), stop=(r == K * NT - 1))
                ins.then_inc(table_done[val], 1)

            pe.wait_ge(lo_ready, 2 * SPLIT)
            for c in range(NC):
                m = slice(c * P, (c + 1) * P)
                product(ps_t[:, c, :], lambda q: w_hi[:, 0, q, m], lambda q: w_lo[:, 0, q, m],
                        lambda q: w_hi[:, 1, q, :], lambda q: w_lo[:, 1, q, :]).then_inc(attn_done, 1)
            pe.wait_ge(silu_done, 1)
            mod_row(2, ROW_SA)
            mod_columns(row_sa, COL_SA)
            transposes(0)
            mod_row(3, ROW_CA)
            mod_columns(row_ca, COL_CA)
            transposes(1)
            mod_row(4, ROW[GA])
            attention(0)
            transposes(2)
            attention(1)
            mod_row(5, ROW[SB])
            transposes(3)
            mod_row(6, ROW[CB])
            attention(2)
            pe.wait_ge(sel_done, 1)
            broadcast(GA, 0)
            transposes(4)
            attention(3)
            broadcast(SB, 1)
            transposes(5)
            attention(4)
            broadcast(CB, 2)
            transposes(6)
            attention(5)
            transposes(7)
            transposes2(0)
            attention(6)
            logits(0)
            transposes2(1)
            attention(7)
            logits(1)
            transposes2(2)
            mod_row(7, ROW[GB])
            logits(2)
            transposes2(3)
            logits(3)
            transposes2(4)
            logits(4)
            transposes2(5)
            broadcast(GB, 3)
            logits(5)
            transposes2(6)
            pe.wait_ge(m_read, M_JOBS)
            for n in range(4):
                ranks(n)
            logits(6)
            transposes2(7)
            ranks(4)
            ranks(5)
            logits(7)
            ranks(6)
            ranks(7)
            t_.matmul(ps_m[0:E, 0, 0:P], before[:, NT, :], ones, start=True, stop=True
                      ).then_inc(total_done, 1)
            pe.wait_ge(over_ready, 1)
            t_.matmul(ps_m[:, 0, 0:E + 1], over[:], upper, start=True, stop=True)
            t_.matmul(ps_m[0:E, 0, 64:65], upper_inc, over[:, 0:1], start=True, stop=True
                      ).then_inc(base_done, 1)
            pe.wait_ge(row_hot_ready, K)
            pe.wait_ge(col_hot_ready[0], 1)
            table(0, 0)
            pe.wait_ge(col_hot_ready[1], 1)
            table(1, 1)
            pe.wait_ge(owner_ready, 1)
            t_.matmul(ps_y[0:1, 0, 0:16], ones[0:E, 0:1], over_cmp[:], start=True, stop=True
                      ).then_inc(owner_done, 1)

            def transpose_rows(e0, u):
                pe.wait_ge(gathered[u % 8], e0 * 2 + 16 * (u // 8 + 1))
                for c in range(NC):
                    ins = t_.transpose(ps_t[:, u % 2, c * P:(c + 1) * P],
                                       ring_g[u % 8][:, c * P:(c + 1) * P], ident)
                ins.then_inc(g_used, 1)

            pe.wait_ge(slots_ready, 2)
            pe.wait_ge(weights_ready, 1)
            transpose_rows(0, 0)
            pe.wait_ge(share_ready, 1)
            for n in range(NT):
                ins = t_.transpose(ps_t[0:E, 2 + n // 4, (n % 4) * P:(n % 4 + 1) * P], prod[:, n, :], ident)
                if n % 4 == 3:
                    ins.then_inc(share_t_done, 1)
            pe.wait_ge(owner_ready, 2)
            pe.wait_ge(share_t_read, 2)
            pe.wait_ge(bexp_landed, 16)
            for n in range(NT):
                if n >= 2:
                    pe.wait_ge(bias_scaled, n - 1)
                t_.matmul(ps_y[:, n % 2, :], share_t[:, n * P:(n + 1) * P], b_exp, start=True, stop=True
                          ).then_inc(bias_done, 1)

            def step(e0, u):
                pe.wait_ge(xt_lo_done, e0 + u + 1)
                transpose_rows(e0, u + 1)
                pe.wait_ge(lo_ready, e0 * 2 + 2 * (SPLIT + u + 1))
                pe.wait_ge(expert_read, e0 + u + 1)
                k, m = u % 2, slice((u % 2) * P, (u % 2 + 1) * P)
                product(ps_m[:, k, :], lambda c: ht_hi[:, c, m], lambda c: ht_lo[:, c, m],
                        lambda c: w_hi[:, k, c, :], lambda c: w_lo[:, k, c, :]).then_inc(expert_done, 1)

            with pe.Fori(0, E // RING) as i:
                for u in range(RING):
                    step(i * RING, u)

            pe.wait_ge(xt_lo_done, E + 1)
            count = pe.value_load(over_count[0:1, 0:1], min_val=0, max_val=NOV)
            with pe.If(count > 0):
                with pe.Fori(0, NOV) as q:
                    with pe.If(count > q):
                        pe.wait_ge(ov_g, 16 * q + 16)
                        for c in range(NC):
                            ins = t_.transpose(ps_t[:, 0, c * P:(c + 1) * P],
                                               ring_g[1][:, c * P:(c + 1) * P], ident)
                        ins.then_inc(ov_t, 1)
                        pe.wait_ge(ov_lo, 2 * q + 2)
                        product(ps_m[:, 0, :], lambda c: ht_hi[:, c, 0:P], lambda c: ht_lo[:, c, 0:P],
                                lambda c: w_hi[:, 0, c, :], lambda c: w_lo[:, 0, c, :]).then_inc(ov_y, 1)
                    with pe.Else():
                        pe.nop()
                    pe.nop()
                pe.nop()
            with pe.Else():
                pe.nop()


def _constants():
    import numpy as np
    c = np.zeros((P, C_ALL), np.float32)
    i = np.arange(P)
    c[:, C_ID:C_ID + P] = i[:, None] == i[None, :]
    c[:, C_TRI:C_TRI + P] = i[:, None] < i[None, :]
    c[:, C_ONE:C_ONE + P] = 1
    c[:, C_IOTA:C_IOTA + P] = i[None, :]
    c[0:E, C_UP:C_UP + E] = i[0:E, None] < i[None, 0:E]
    c[0:E, C_UP + E] = 1
    c[0:E, C_INC:C_INC + E] = i[0:E, None] <= i[None, 0:E]
    r = np.arange(K * NT)
    c[:, C_PID:C_PID + K * NT] = r[None, :] * P + i[:, None] + 1
    for b in range(NB):
        c[b, C_SEL + b * P:C_SEL + (b + 1) * P] = 1
    return c


def kernel(L0_attn_x, L0_attn_w1, L0_attn_w2, L0_attn_b2, L0_attn_sparse_mask, L0_ffn_gate_w,
           L0_ffn_expert_w, L0_ffn_expert_b, L0_c, L0_wmod):
    import numpy as np
    import concourse.bacc as bacc
    from concourse.bass_utils import run_bass_kernel_spmd

    def chunked(a):
        return np.ascontiguousarray(a.reshape(NC, P, -1).transpose(1, 0, 2).reshape(P, -1))

    a = {k: np.asarray(v) for k, v in dict(
        x=L0_attn_x, w1=L0_attn_w1, w2=L0_attn_w2, b2=L0_attn_b2, mask=L0_attn_sparse_mask,
        gate=L0_ffn_gate_w, wexp=L0_ffn_expert_w, bexp=L0_ffn_expert_b, c=L0_c, wmod=L0_wmod).items()}
    arrays = {
        "in_x": a["x"].reshape(T, D),
        "in_w1": a["w1"],
        "in_w2t": np.ascontiguousarray(a["w2"].T),
        "in_b2": a["b2"],
        "in_maskt": chunked(a["mask"].T),
        "in_gatet": chunked(a["gate"].T),
        "in_wexp": np.ascontiguousarray(
            a["wexp"].reshape(E, D, NC, P).transpose(0, 3, 2, 1).reshape(E, P, UNIT)),
        "in_bexp": a["bexp"],
        "in_ct": np.ascontiguousarray(a["c"].T).reshape(P, NC * NB),
        "in_wmod": a["wmod"],
        "in_consts": _constants(),
    }
    nc = bacc.Bacc("TRN2", target_bir_lowering=False, num_devices=1)
    args = [nc.dram_tensor(n, v.shape, mybir.dt.from_np(v.dtype), kind="ExternalInput").ap()
            for n, v in arrays.items()]
    out = nc.dram_tensor("out_0", (NB, PAIR * P, D), F32, kind="ExternalOutput").ap()
    adaln_moe(nc, *args, out)
    r = run_bass_kernel_spmd(nc, [arrays], core_ids=[0])
    return r.results[0]["out_0"]
```

```python
from contextlib import ExitStack

import concourse.bass as bass
from concourse import mybir

F32 = mybir.dt.float32
F32R = mybir.dt.float32r
I32 = mybir.dt.int32
U32 = mybir.dt.uint32
ALU = mybir.AluOpType
ACT = mybir.ActivationFunctionType
AX_X = mybir.AxisListType.X

P = 128
D = 512
NC = D // P
T = 1024
NT = T // P
NB = 4
PAIR = NT // NB
E = 32
K = 2
S = 96
DIV_MUL, DIV_SHIFT = 683, 16
NOV = (K * T - 1) // S
NCOL = 56
RING = 10
TURNS = E // RING
REST = E % RING
UNIT = NC * D
FIRST = 8
SPLIT = 2
GA, SB, CB, GB = range(4)
ROW_SA, ROW_CA, COL_SA, COL_CA = range(4)
ROW = {GA: 4, SB: 5, CB: 6, GB: 7}
M_JOBS = 8
Y_RING = 10
SHARE_STEPS = (1, 6)
AHEAD = 9
EPS = 1e-5
EMPTY = 4096.0

C_ID, C_TRI, C_ONE, C_IOTA = 0, 128, 256, 384
C_UP, C_INC, C_PID = 512, 512 + E + 1, 512 + 2 * E + 1
C_ALL = C_PID + K * NT


def adaln_moe(nc, x, w1, w2t, b2, maskt, gatet, wexp, bexp, ct, wmod, consts, out):
    ctx = ExitStack()
    with ctx:
        def sb(name, shape, dt=F32):
            return ctx.enter_context(nc.sbuf_tensor(name, shape, dt))

        def psum(name, shape):
            return ctx.enter_context(nc.psum_tensor(name, shape, F32))

        def sem(name):
            return ctx.enter_context(nc.semaphore(name))

        h2_rows = nc.dram_tensor("h2_rows", [T, D], F32).ap()
        y_rows = nc.dram_tensor("y_rows", [K * T, D], F32).ap()
        mod_rows = nc.dram_tensor("mod_rows", [4, NB, D], F32).ap()

        raw = sb("raw", [P, FIRST, UNIT])
        w_hi = sb("w_hi", [P, 2, NC, D], F32R)
        w_lo = sb("w_lo", [P, 2, NC, D], F32R)
        attn_hi = sb("attn_hi", [P, NC, D], F32R)
        attn_lo = sb("attn_lo", [P, NC, D], F32R)
        ht_hi = sb("ht_hi", [P, NC, PAIR * P], F32R)
        ht_lo = sb("ht_lo", [P, NC, PAIR * P], F32R)
        xs = sb("xs", [P, NT, D])
        norm = sb("norm", [P, PAIR, D])
        act = sb("act", [P, PAIR, D])
        h2 = sb("h2", [P, PAIR, D])
        bc = sb("bc", [P, 4, NB, D])
        g = sb("g", [P, 4, D])
        y_more = sb("y_more", [P, 3, D])
        cst = sb("cst", [P, C_ALL])
        b2_bc = sb("b2_bc", [P, D])
        gate = sb("gate", [P, NC, E])
        c_raw = sb("c_raw", [P, NC, NB])
        c_silu = sb("c_silu", [P, NC, NB])
        mod_col = sb("mod_col", [P, 2, NC, NB])
        stats = sb("stats", [P, NT, 6])
        mv = sb("mv", [P, NT, 2])
        rstd = sb("rstd", [P, NT])
        half = sb("half", [P, NT])
        mv2 = sb("mv2", [P, NT, 2])
        rstd2 = sb("rstd2", [P, NT])
        logit = sb("logit", [P, E])
        top = sb("top", [P, NT, 8])
        top_at = sb("top_at", [P, PAIR, 8], U32)
        top_e = sb("top_e", [P, K, NT])
        hot = sb("hot", [P, K, NT, E])
        before = sb("before", [P, NT + 1, E])
        prod = sb("prod", [P, NT, E])
        place = sb("place", [P, K, NT])
        weight = sb("weight", [P, K, NT])
        w_tmp = sb("w_tmp", [P, 3, NT])
        over_base = sb("over_base", [P, E + 1])
        over_end = sb("over_end", [E, 1])
        over_cmp = sb("over_cmp", [E, NOV])
        over_expert = sb("over_expert", [1, NOV], I32)
        over_count = sb("over_count", [1, 1], I32)
        gather_at = sb("gather_at", [S, NCOL], U32)
        scatter_at = sb("scatter_at", [S, NCOL], U32)
        over_at = sb("over_at", [S, 2], U32)
        mod_tmp = act[0:NB, :, :]
        row_sa, row_ca = bc[0:NB, GB, 2, :], bc[0:NB, GB, 1, :]
        row_of = [bc[0:NB, n, 3, :] for n in range(4)]
        ring_g = [h[0:S, c, :].bitcast(F32) for h in (attn_hi, attn_lo) for c in range(NC)] + [
            norm[0:S, t, :] for t in range(PAIR)]
        over_i = act[0:E, 0, 0:2 * P].bitcast(I32).rearrange("p (a m) -> p a m", a=2)
        over = act[0:E, 0, 2 * P:3 * P]
        place_f = act[:, 0, 3 * P:3 * P + 7 * K * NT].rearrange("p (a k n) -> p a k n", a=7, k=K)
        slot_f = act[0:S, 1, 0:3 * NCOL].rearrange("p (a n) -> p a n", a=3)
        place_i = act[:, 1, 3 * NCOL:3 * NCOL + 5 * K * NT].bitcast(I32).rearrange(
            "p (a k n) -> p a k n", a=5, k=K)
        rank = act[:, 1, 256:256 + NT * E].rearrange("p (n e) -> p n e", n=NT)
        ring_y = [g[0:S, n, :] for n in range(4)] + [act[0:S, t, :] for t in range(PAIR)] + [
            h2[0:S, 1, :]] + [y_more[0:S, n, :] for n in range(3)]
        bias_row = h2[:, 0, :]
        row_hot = [h[:, :, :].rearrange("p c m -> p (c m)")[:, 0:NT * S].rearrange("p (n m) -> p n m", m=S)
                   for h in (ht_hi, ht_lo)]
        col_hot = attn_hi[:, 0:2, :].rearrange("p c d -> p (c d)")[:, 0:K * NT * NCOL].rearrange(
            "p (r m) -> p r m", m=NCOL)
        col_one = g[:, 2:4, :].rearrange("p a d -> p (a d)")[:, 0:K * NT * NCOL].rearrange(
            "p (r m) -> p r m", m=NCOL)
        ranked = norm[:, 0, :].rearrange("p (k n e) -> p k n e", k=K, n=NT)
        share, share_tmp = (norm[:, 1, h * NT * E:(h + 1) * NT * E].rearrange("p (n e) -> p n e", n=NT)
                            for h in range(2))
        share_t = bc[0:E, 0, 0:2, :].rearrange("p a d -> p (a d)")
        b_exp = bc[0:E, 0, 2, :]
        share_now = bc[0:E, 0, 3, 0:PAIR * P].rearrange("p (a m) -> p a m", a=PAIR)

        ps_t = psum("ps_t", [P, 4, 512])
        ps_y = psum("ps_y", [P, 2, 512])
        ps_m = psum("ps_m", [P, 2, 512])

        def gathered_t(k):
            return ps_t[:, k, :].rearrange("p (c m) -> p c m", c=NC)[:, :, 0:S]

        def column_part(part, k):
            return part[:, :, k * P:k * P + S]

        ident = cst[:, C_ID:C_ID + P]
        tri = cst[:, C_TRI:C_TRI + P]
        ones = cst[:, C_ONE:C_ONE + P]
        iota = cst[:, C_IOTA:C_IOTA + P]
        upper = cst[0:E, C_UP:C_UP + E + 1]
        upper_inc = cst[0:E, C_INC:C_INC + E]
        pair_id = cst[:, C_PID:C_PID + K * NT].rearrange("p (k n) -> p k n", k=K)

        c_landed = sem("c_landed")
        consts_landed = sem("consts_landed")
        params_landed = sem("params_landed")
        raw_landed = [sem(f"raw_landed{s}") for s in range(RING)]
        half_landed = [sem(f"half_landed{j}") for j in range(SPLIT)]
        x_landed = [sem(f"x_landed{s}") for s in range(2)]
        mask_landed = sem("mask_landed")
        h2_written = [sem(f"h2_written{s}") for s in range(2)]
        bexp_landed = sem("bexp_landed")
        silu_done = sem("silu_done")
        hi_ready = sem("hi_ready")
        lo_ready = sem("lo_ready")
        m_done = sem("m_done")
        m_read = sem("m_read")
        gains_ready = sem("gains_ready")
        mod_stored = [sem(f"mod_stored{n}") for n in range(4)]
        mod_landed = [sem(f"mod_landed{n}") for n in range(4)]
        attn_done = sem("attn_done")
        attn_read = sem("attn_read")
        attn_hi_done = sem("attn_hi_done")
        attn_lo_done = sem("attn_lo_done")
        stats_done = sem("stats_done")
        half_done = sem("half_done")
        rstd_done = sem("rstd_done")
        norm_ready = sem("norm_ready")
        t_done = sem("t_done")
        ht_ready = sem("ht_ready")
        ht_hi_done = sem("ht_hi_done")
        ht_lo_done = sem("ht_lo_done")
        y_done = sem("y_done")
        y_read = sem("y_read")
        gelu_done = sem("gelu_done")
        x2_ready = sem("x2_ready")
        stats2_done = sem("stats2_done")
        rstd2_done = sem("rstd2_done")
        h2_ready = sem("h2_ready")
        t2_done = sem("t2_done")
        h2t_ready = sem("h2t_ready")
        logits_done = sem("logits_done")
        logits_read = sem("logits_read")
        picks_ready = sem("picks_ready")
        ranks_done = sem("ranks_done")
        total_done = sem("total_done")
        over_ready = sem("over_ready")
        base_done = sem("base_done")
        base_read = sem("base_read")
        owner_done = sem("owner_done")
        owner_ready = sem("owner_ready")
        exp_in = sem("exp_in")
        exp_done = sem("exp_done")
        weight_ready = sem("weight_ready")
        place_ready = sem("place_ready")
        row_hot_ready = sem("row_hot_ready")
        col_one_ready = sem("col_one_ready")
        col_hot_ready = sem("col_hot_ready")
        table_done = sem("table_done")
        slots_ready = sem("slots_ready")
        share_ready = sem("share_ready")
        share_t_done = sem("share_t_done")
        share_t_read = sem("share_t_read")
        share_picked = sem("share_picked")
        bias_done = sem("bias_done")
        bias_scaled = sem("bias_scaled")
        bias_added = sem("bias_added")
        gathered = [sem(f"gathered{s}") for s in range(RING)]
        g_used = sem("g_used")
        xt_hi_done = sem("xt_hi_done")
        xt_lo_done = sem("xt_lo_done")
        half_used = sem("half_used")
        expert_done = sem("expert_done")
        expert_read = sem("expert_read")
        scattered = [sem(f"scattered{s}") for s in range(Y_RING)]
        ov_w = sem("ov_w")
        ov_at = sem("ov_at")
        ov_g = sem("ov_g")
        ov_t = sem("ov_t")
        ov_hi = sem("ov_hi")
        ov_lo = sem("ov_lo")
        ov_y = sem("ov_y")
        ov_out = sem("ov_out")
        rows_left = sem("rows_left")
        ov_turn = sem("ov_turn")
        ov_done = sem("ov_done")
        rows_complete = sem("rows_complete")
        rows_landed = [sem(f"rows_landed{n}") for n in range(NT)]
        second_ready = sem("second_ready")
        sum_ready = sem("sum_ready")
        out_ready = sem("out_ready")
        last_ready = sem("last_ready")
        stored = sem("stored")
        dve_chain = sem("dve_chain")
        pool_chain = sem("pool_chain")

        def unit_source(j):
            if j >= 2:
                return wmod.rearrange("(p c) n -> p c n", c=NC)[:, :, (j - 2) * D:(j - 1) * D]
            return (w1, w2t)[j].rearrange("(p c) n -> p c n", c=NC)

        def slot(s):
            return raw[:, s, :] if s < FIRST else bc[:, (SB, CB)[s - FIRST], :, :].rearrange("p b d -> p (b d)")

        def slot3(s):
            return slot(s).rearrange("p (c n) -> p c n", c=NC)

        block = ctx.enter_context(nc.Block())

        @block.sync
        def _(sp):
            sp.dma_start(c_raw[:], ct.rearrange("p (c b) -> p c b", c=NC)).then_inc(c_landed, 16)

            def load_unit(j):
                sp.dma_start(slot3(j), unit_source(j)).then_inc(raw_landed[j], 16)

            for h in range(2):
                for j in range(SPLIT):
                    c = slice(2 * h, 2 * h + 2)
                    sp.dma_start(slot3(j)[:, c, :], unit_source(j)[:, c, :]
                                 ).then_inc((half_landed, raw_landed)[h][j], 16)
            sp.dma_start(g[:], maskt.rearrange("p (c n) -> p c n", c=NC)).then_inc(mask_landed, 16)
            sp.dma_start(cst[:], consts).then_inc(consts_landed, 16)
            x_v = x.rearrange("(n p) d -> p n d", p=P)
            for s in range(2):
                n = slice(s * NT // 2, (s + 1) * NT // 2)
                sp.dma_start(xs[:, n, :], x_v[:, n, :]).then_inc(x_landed[s], 16)
            load_unit(2)
            load_unit(3)
            sp.dma_start(b2_bc[:], b2.rearrange("(a n) -> a n", a=1).broadcast_to([P, D])
                         ).then_inc(params_landed, 16)
            sp.dma_start(gate[:], gatet.rearrange("p (c n) -> p c n", c=NC)).then_inc(params_landed, 16)
            for j in range(4, FIRST - 1):
                load_unit(j)

            def load_expert(e, u):
                sp.dma_start(slot(u), wexp[bass.ds(e, 1), :, :].rearrange("a p n -> (a p) n")
                             ).then_inc(raw_landed[u], 16)

            def store_h2(n):
                sp.wait_ge(h2_ready, n + 1)
                sp.dma_start(h2_rows[n * P:(n + 1) * P, :], h2[:, n % 2, :]).then_inc(h2_written[n % 2], 16)

            def store_mod(n):
                if n == GA:
                    sp.wait_ge(gains_ready, 1)
                else:
                    sp.wait_ge(m_read, ROW[n] + 1)
                sp.dma_start(mod_rows[n], row_of[n]).then_inc(mod_stored[n], 16)

            def broadcast(n):
                sp.wait_ge(mod_stored[n], 16)
                sp.dma_start(bc[:, n, :, :].rearrange("p b d -> p (b d)"),
                             mod_rows[n:n + 1].rearrange("a b d -> a (b d)").broadcast_to([P, NB * D])
                             ).then_inc(mod_landed[n], 16)

            def reload(u, job):
                sp.wait_ge(m_done, job + 1)
                load_expert(u, u)

            store_mod(GA)
            load_unit(FIRST - 1)
            broadcast(GA)
            sp.wait_ge(lo_ready, 2 * SPLIT)
            load_expert(0, 0)
            load_expert(1, 1)
            store_mod(SB)
            reload(2, ROW_SA)
            broadcast(SB)
            store_mod(CB)
            reload(3, ROW_CA)
            broadcast(CB)
            reload(4, ROW[GA])
            for n in range(NT):
                store_h2(n)
                if n in (1, 3, 5):
                    u = 5 + n // 2
                    reload(u, {5: ROW[SB], 6: ROW[CB], 7: ROW[GB]}[u])
            for u in range(FIRST, RING):
                load_expert(u, u)
            with sp.Fori(1, TURNS) as i:
                for u in range(RING):
                    sp.wait_ge(lo_ready, i * (2 * RING) + 2 * (SPLIT + u + 1 - RING))
                    load_expert(i * RING + u, u)
            for u in range(REST):
                sp.wait_ge(lo_ready, 2 * (SPLIT + (TURNS - 1) * RING + u + 1))
                load_expert(TURNS * RING + u, u)

            sp.wait_ge(owner_ready, 2)
            count = sp.value_load(over_count[0:1, 0:1], min_val=0, max_val=NOV)
            sp.wait_ge(lo_ready, 2 * (SPLIT + E))
            with sp.If(count > 0):
                with sp.Fori(0, NOV) as q:
                    with sp.If(count > q):
                        owner = sp.value_load(over_expert[0:1, bass.ds(q, 1)], min_val=0, max_val=E - 1)
                        sp.wait_ge(ov_done, q + 1)
                        sp.dma_start(raw[:, 0, :], wexp[bass.ds(owner, 1), :, :].rearrange(
                            "a p n -> (a p) n")).then_inc(ov_w, 16)
                    with sp.Else():
                        sp.nop()
                    sp.nop()
                sp.nop()
            with sp.Else():
                sp.nop()
            sp.wait_ge(rows_complete, 1)
            y_v = y_rows.rearrange("(k n p) d -> n p k d", p=P, k=K)
            for n in range(NT):
                sp.dma_start(raw[:, n, 0:K * D].rearrange("p (k d) -> p k d", k=K), y_v[n]
                             ).then_inc(rows_landed[n], 16)
            out_v = out.rearrange("b (a p) d -> (b a) p d", p=P)
            for n in range(NT):
                if n < NT - 1:
                    sp.wait_ge(out_ready, n + 1)
                else:
                    sp.wait_ge(last_ready, 1)
                sp.dma_start(out_v[n], xs[:, n, :]).then_inc(stored, 16)
            sp.wait_ge(stored, 16 * NT)

        @block.scalar
        def _(a):
            s = nc.scalar
            a.wait_ge(c_landed, 16)
            s.activation(c_silu[:], c_raw[:], ACT.Silu).then_inc(silu_done, 1)

            def split_hi(u, slot, h):
                c = slice(2 * h, 2 * h + 2)
                s.copy(w_hi[:, u % 2, c, :], slot3(slot)[:, c, :]).then_inc(hi_ready, 1)

            def read_m(job, dst, src):
                a.wait_ge(m_done, job + 1)
                s.copy(dst, src).then_inc(m_read, 1)

            def read_row(job, dst):
                read_m(job, dst, ps_m[0:NB, job % 2, :])

            def read_row_plus_1(job, dst):
                a.wait_ge(m_done, job + 1)
                s.activation(dst, ps_m[0:NB, job % 2, :], ACT.Copy, bias=1.0).then_inc(m_read, 1)

            def read_col(job, n):
                read_m(job, mod_col[:, n, :, :].rearrange("p c b -> p (c b)"), ps_m[:, job % 2, 0:NC * NB])

            def modulate(n):
                a.wait_ge(t_done, n + 1)
                if n == 0:
                    a.wait_ge(m_read, COL_CA + 1)
                b = n // PAIR
                nt = norm[:, n % 2, :].rearrange("p (c m) -> p c m", c=NC)
                for c in range(NC):
                    s.activation(nt[:, c, :], ps_t[:, n % 2, c * P:(c + 1) * P], ACT.Identity,
                                 bias=mod_col[:, 0, c, b:b + 1], scale=mod_col[:, 1, c, b:b + 1]
                                 ).then_inc(ht_ready, 1)
                if n >= 2:
                    a.wait_ge(y_done, n - 1)
                a.wait_ge(ht_ready, NC * (n + 1))
                s.copy(ht_hi[:, :, (n % 2) * P:(n % 2 + 1) * P], nt).then_inc(ht_hi_done, 1)

            def gelu(n):
                a.wait_ge(y_read, n + 1)
                s.activation(act[:, n % 2, :], act[:, n % 2, :], ACT.Gelu).then_inc(gelu_done, 1)

            def copy_h2t(n):
                a.wait_ge(t2_done, n + 1)
                if n >= 2:
                    a.wait_ge(logits_done, n - 1)
                s.copy(g[:, n % 2, :], ps_t[:, 2 + n % 2, :]).then_inc(h2t_ready, 1)

            def expert_hi(i, u, h):
                if isinstance(i, int) and i * RING + u < 2:
                    a.wait_ge(attn_done, NC)
                else:
                    a.wait_ge((half_used, expert_done)[h], i * RING + u)
                if h == 0:
                    before = u // RING + (u % RING < FIRST)
                    a.wait_ge(raw_landed[u % RING], i * 16 + 16 * (before + 1))
                split_hi(u, u % RING, h)

            for h in range(2):
                for j in range(SPLIT):
                    a.wait_ge((half_landed, raw_landed)[h][j], 16)
                    split_hi(j, j, h)
            for c in range(NC):
                a.wait_ge(attn_read, c + 1)
                s.copy(attn_hi[:, c, :], h2[:, c % 2, :]).then_inc(attn_hi_done, 1)
                if c == 1:
                    read_row(ROW_SA, row_sa)
            read_row_plus_1(ROW_CA, row_ca)
            read_col(COL_SA, 0)
            read_col(COL_CA, 1)
            modulate(0)
            modulate(1)
            read_row(ROW[GA], row_of[GA])
            modulate(2)
            gelu(0)
            read_row(ROW[SB], row_of[SB])
            modulate(3)
            gelu(1)
            read_row_plus_1(ROW[CB], row_of[CB])
            modulate(4)
            gelu(2)
            for u in range(2):
                for h in range(2):
                    expert_hi(0, u, h)
            modulate(5)
            gelu(3)
            read_row(ROW[GB], row_of[GB])
            modulate(6)
            gelu(4)
            modulate(7)
            copy_h2t(0)
            gelu(5)
            copy_h2t(1)
            gelu(6)
            copy_h2t(2)
            gelu(7)
            copy_h2t(3)
            copy_h2t(4)
            copy_h2t(5)
            copy_h2t(6)
            copy_h2t(7)
            a.wait_ge(x2_ready, NT)
            a.dma_start(b_exp, bexp).then_inc(bexp_landed, 16)
            a.wait_ge(gains_ready, 2)
            a.dma_start(mod_rows[GB], row_of[GB]).then_inc(mod_stored[GB], 16)
            a.wait_ge(exp_in, 1)
            s.activation(w_tmp[:, 1, :], w_tmp[:, 0, :], ACT.Exp).then_inc(exp_done, 1)
            a.wait_ge(mod_stored[GB], 16)
            a.dma_start(bc[:, GB, :, :].rearrange("p b d -> p (b d)"),
                        mod_rows[GB:GB + 1].rearrange("a b d -> a (b d)").broadcast_to([P, NB * D])
                        ).then_inc(mod_landed[GB], 16)
            for h in range(2):
                a.wait_ge(share_t_done, h + 1)
                s.copy(share_t[:, h * 512:(h + 1) * 512], ps_t[0:E, 2 + h, :]).then_inc(share_t_read, 1)

            def rows_hi(e0, u):
                a.wait_ge(g_used, e0 + u + 1)
                a.wait_ge(expert_done, e0 + u)
                k = u % 2
                s.copy(column_part(ht_hi, k), gathered_t(k)).then_inc(xt_hi_done, 1)

            def rows_out(e0, u):
                a.wait_ge(expert_done, e0 + u + 2)
                a.wait_ge(rows_left, e0 + u + 1)
                s.copy(ring_y[u % Y_RING], ps_m[0:S, u % 2, :]).then_inc(expert_read, 1)

            def pick_share(i, j):
                a.wait_ge(bias_done, i * PAIR + j + 1)
                s.copy(share_now[:, j, :], share_t[:, bass.ds(i * (PAIR * P) + j * P, P)]
                       ).then_inc(share_picked, 1)

            def step(i, u):
                expert_hi(i, u + 2, 0)
                rows_out(i * RING, u)
                rows_hi(i * RING, u + 2)
                expert_hi(i, u + 2, 1)

            a.wait_ge(share_t_read, 2)
            for k in range(2):
                a.wait_ge(g_used, k + 1)
                s.copy(column_part(ht_hi, k), gathered_t(k)).then_inc(xt_hi_done, 1)
            with a.Fori(0, TURNS) as i:
                for u in range(RING):
                    step(i, u)
                    if u in SHARE_STEPS:
                        pick_share(i, SHARE_STEPS.index(u))
            for j in range(PAIR):
                pick_share(TURNS, j)
            for u in range(REST):
                rows_out(TURNS * RING, u)

            count = a.value_load(over_count[0:1, 0:1], min_val=0, max_val=NOV)
            with a.If(count > 0):
                with a.Fori(0, NOV) as q:
                    with a.If(count > q):
                        a.wait_ge(ov_w, 16 * q + 16)
                        s.copy(w_hi[:, 0, :, :], slot3(0)).then_inc(ov_hi, 1)
                        a.wait_ge(ov_t, q + 1)
                        s.copy(column_part(ht_hi, 0), gathered_t(0)).then_inc(ov_hi, 1)
                        a.wait_ge(ov_y, q + 1)
                        s.copy(act[0:S, 0, :], ps_m[0:S, 0, :]).then_inc(ov_out, 1)
                    with a.Else():
                        a.nop()
                    a.nop()
                a.nop()
            with a.Else():
                a.nop()

            for n in range(NT):
                a.wait_ge(rows_landed[n], 16)
                s.activation(raw[:, n, D:2 * D], raw[:, n, D:2 * D], ACT.Copy, scale=weight[:, 1, n:n + 1]
                             ).then_inc(second_ready, 1)

        @block.vector
        def _(v):
            d = nc.vector
            linked = [0]

            def link(ins):
                linked[0] += 1
                ins.then_inc(dve_chain, 1)
                v.wait_ge(dve_chain, linked[0])

            def split_lo(j, slot, h, before):
                c = slice(2 * h, 2 * h + 2)
                v.wait_ge(hi_ready, before + 1)
                d.tensor_tensor(w_lo[:, j % 2, c, :], slot3(slot)[:, c, :],
                                w_hi[:, j % 2, c, :].bitcast(F32), ALU.subtract).then_inc(lo_ready, 1)

            def expert_lo(i, u, halves=range(2)):
                for h in halves:
                    split_lo(u, u % RING, h, i * (2 * RING) + 2 * (SPLIT + u) + h)

            def norm_stats(m, n, done):
                link(d.bn_stats(stats[:, n, :], xs[:, n, :]))
                d.bn_aggr(m[:, n, :], stats[:, n, :]).then_inc(done, 1)

            def norm_rows(n):
                if n >= 2:
                    v.wait_ge(ht_lo_done, n - 1)
                d.tensor_scalar(norm[:, n % 2, :], xs[:, n, :], mv[:, n, 0:1], rstd[:, n:n + 1],
                                ALU.subtract, ALU.mult).then_inc(norm_ready, 1)

            def mask_attn(c):
                v.wait_ge(attn_done, c + 1)
                if c >= 2:
                    v.wait_ge(attn_lo_done, c - 1)
                d.tensor_tensor(h2[:, c % 2, :], ps_t[:, c, :], g[:, c, :], ALU.mult).then_inc(attn_read, 1)

            def attn_lo_part(c):
                v.wait_ge(attn_hi_done, c + 1)
                d.tensor_tensor(attn_lo[:, c, :], h2[:, c % 2, :], attn_hi[:, c, :].bitcast(F32),
                                ALU.subtract).then_inc(attn_lo_done, 1)

            def ht_lo_part(n):
                v.wait_ge(ht_hi_done, n + 1)
                m = slice((n % 2) * P, (n % 2 + 1) * P)
                d.tensor_tensor(ht_lo[:, :, m], norm[:, n % 2, :].rearrange("p (c m) -> p c m", c=NC),
                                ht_hi[:, :, m].bitcast(F32), ALU.subtract).then_inc(ht_lo_done, 1)

            def add_b2(n):
                v.wait_ge(y_done, n + 1)
                if n >= 2:
                    v.wait_ge(x2_ready, n - 1)
                d.tensor_tensor(act[:, n % 2, :], ps_y[:, n % 2, :], b2_bc[:], ALU.add).then_inc(y_read, 1)

            def bound_gain(n, turn):
                v.wait_ge(m_read, ROW[n] + 1)
                row = row_of[n]
                link(d.tensor_scalar(mod_tmp[:, 0, :], row, 0.0, 2.0, ALU.is_ge, ALU.mult))
                link(d.tensor_scalar(mod_tmp[:, 0, :], mod_tmp[:, 0, :], -1.0, None, ALU.add))
                link(d.scalar_tensor_tensor(out=mod_tmp[:, 1, :], in0=row, scalar=-1.0, in1=row,
                                            op0=ALU.mult, op1=ALU.max))
                d.scalar_tensor_tensor(out=row, in0=mod_tmp[:, 1, :], scalar=0.25, in1=mod_tmp[:, 0, :],
                                       op0=ALU.max, op1=ALU.mult).then_inc(gains_ready, 1)
                v.wait_ge(gains_ready, turn + 1)

            def second_stats(n):
                v.wait_ge(x2_ready, n + 1)
                norm_stats(mv2, n, stats2_done)

            def scale_rows(n):
                v.wait_ge(rstd2_done, n + 1)
                b, row = n // PAIR, h2[:, n % 2, :]
                if n < 2:
                    v.wait_ge(attn_lo_done, NC)
                    v.wait_ge(mod_landed[SB], 16)
                    v.wait_ge(mod_landed[CB], 16)
                else:
                    v.wait_ge(t2_done, n - 1)
                    v.wait_ge(h2_written[n % 2], 16 * (n // 2))
                link(d.scalar_tensor_tensor(out=row, in0=xs[:, n, :], scalar=mv2[:, n, 0:1],
                                            in1=bc[:, CB, b, :], op0=ALU.subtract, op1=ALU.mult))
                d.scalar_tensor_tensor(out=row, in0=row, scalar=rstd2[:, n:n + 1], in1=bc[:, SB, b, :],
                                       op0=ALU.mult, op1=ALU.add).then_inc(h2_ready, 1)

            def pick(n):
                v.wait_ge(logits_done, n + 1)
                link(d.max(top[:, n, :], ps_t[:, 2 + n % 2, 0:E]))
                d.max_index(top_at[:, n % 2, :], top[:, n, :], ps_t[:, 2 + n % 2, 0:E]).then_inc(logits_read, 1)

            def pick_hot(b):
                n = slice(PAIR * b, PAIR * (b + 1))
                v.wait_ge(logits_read, PAIR * (b + 1))
                link(d.tensor_copy(top_e[:, :, n].rearrange("p k n -> p n k"), top_at[:, :, 0:K]))
                link(d.tensor_tensor(hot[:, :, n, :],
                                     iota[:, 0:E].unsqueeze(1).unsqueeze(1).broadcast_to([P, K, PAIR, E]),
                                     top_e[:, :, n].unsqueeze(3).broadcast_to([P, K, PAIR, E]), ALU.is_equal))
                link(d.tensor_tensor(prod[:, n, :], hot[:, 0, n, :], hot[:, 1, n, :], ALU.add))
                for m in range(PAIR * b, PAIR * (b + 1)):
                    d.tensor_tensor(before[:, m + 1, :], before[:, m, :], prod[:, m, :], ALU.add
                                    ).then_inc(picks_ready, 1)
                    v.wait_ge(picks_ready, m + 1)

            link(d.memset(before[:, 0, :], 0.0))
            for h in range(2):
                for j in range(SPLIT):
                    split_lo(j, j, h, 2 * h + j)
            v.wait_ge(x_landed[0], 16)
            for n in range(NT // 2):
                norm_stats(mv, n, stats_done)
            v.wait_ge(mask_landed, 16)
            mask_attn(0)
            mask_attn(1)
            attn_lo_part(0)
            mask_attn(2)
            attn_lo_part(1)
            mask_attn(3)
            attn_lo_part(2)
            v.wait_ge(rstd_done, 1)
            norm_rows(0)
            attn_lo_part(3)
            norm_rows(1)
            v.wait_ge(x_landed[1], 16)
            for n in range(NT // 2, NT):
                norm_stats(mv, n, stats_done)
            ht_lo_part(0)
            ht_lo_part(1)
            norm_rows(2)
            norm_rows(3)
            bound_gain(GA, 0)
            v.wait_ge(params_landed, 2 * 16)
            add_b2(0)
            ht_lo_part(2)
            v.wait_ge(rstd_done, 2)
            norm_rows(4)
            add_b2(1)
            ht_lo_part(3)
            norm_rows(5)
            add_b2(2)
            ht_lo_part(4)
            expert_lo(0, 0)
            expert_lo(0, 1)
            norm_rows(6)
            second_stats(0)
            add_b2(3)
            second_stats(1)
            ht_lo_part(5)
            norm_rows(7)
            add_b2(4)
            second_stats(2)
            scale_rows(0)
            ht_lo_part(6)
            add_b2(5)
            second_stats(3)
            scale_rows(1)
            ht_lo_part(7)
            add_b2(6)
            second_stats(4)
            scale_rows(2)
            add_b2(7)
            pick(0)
            second_stats(5)
            scale_rows(3)
            pick(1)
            pick_hot(0)
            second_stats(6)
            scale_rows(4)
            pick(2)
            second_stats(7)
            scale_rows(5)
            pick(3)
            pick_hot(1)
            scale_rows(6)
            pick(4)
            scale_rows(7)
            pick(5)
            pick_hot(2)
            bound_gain(GB, 1)
            pick(6)
            pick(7)
            pick_hot(3)

            d.tensor_tensor(w_tmp[:, 0, :], top[:, :, 1], top[:, :, 0], ALU.subtract).then_inc(exp_in, 1)
            v.wait_ge(total_done, 1)
            link(d.tensor_scalar(over_i[:, 0, :], ps_m[0:E, 0, 0:P], float(S - 1), float(DIV_MUL),
                                 ALU.add, ALU.mult))
            link(d.tensor_scalar(over_i[:, 1, :], over_i[:, 0, :], DIV_SHIFT, None, ALU.arith_shift_right))
            d.tensor_scalar(over[:], over_i[:, 1, :], -1.0, 0.0, ALU.add, ALU.max).then_inc(over_ready, 1)
            v.wait_ge(exp_done, 1)
            link(d.tensor_scalar(w_tmp[:, 2, :], w_tmp[:, 1, :], 1.0, None, ALU.add))
            link(d.reciprocal(weight[:, 0, :], w_tmp[:, 2, :]))
            d.tensor_tensor(weight[:, 1, :], w_tmp[:, 1, :], weight[:, 0, :], ALU.mult
                            ).then_inc(weight_ready, 1)
            v.wait_ge(base_done, 1)
            d.tensor_copy(over_base[:], ps_m[:, 0, 0:E + 1]).then_inc(base_read, 1)
            d.tensor_copy(over_end[:], ps_m[0:E, 0, 64:65]).then_inc(base_read, 1)
            v.wait_ge(base_read, 2)
            v.wait_ge(ranks_done, NT)
            base = over_base[:, 0:E].unsqueeze(1).broadcast_to([P, NT, E])
            link(d.scalar_tensor_tensor(out=rank[:], in0=base, scalar=float(T),
                                        in1=ps_m[:, 1, 0:NT * E].rearrange("p (n e) -> p n e", n=NT),
                                        op0=ALU.mult, op1=ALU.add))
            rank_k = rank[:].unsqueeze(1).broadcast_to([P, K, NT, E])
            link(d.tensor_tensor(ranked[:], rank_k, hot[:], ALU.mult))
            link(d.tensor_reduce(place[:], ranked[:], AX_X, ALU.add))
            BOTH, RANK, OVER, SCALED, CHUNK = range(5)
            f_rank, f_chunk, f_over, f_row, f_is, f_col, f_sum = (place_f[:, i] for i in range(7))
            link(d.tensor_copy(place_i[:, BOTH], place[:]))
            link(d.tensor_scalar(place_i[:, RANK], place_i[:, BOTH], T - 1, None, ALU.bitwise_and))
            link(d.tensor_scalar(place_i[:, SCALED], place_i[:, RANK], float(DIV_MUL), None, ALU.mult))
            d.tensor_scalar(place_i[:, OVER], place_i[:, BOTH], 10, None, ALU.arith_shift_right)
            d.tensor_copy(f_rank, place_i[:, RANK])
            link(d.tensor_scalar(place_i[:, CHUNK], place_i[:, SCALED], DIV_SHIFT, None,
                                 ALU.arith_shift_right))
            d.tensor_copy(f_over, place_i[:, OVER])
            link(d.tensor_copy(f_chunk, place_i[:, CHUNK]))
            link(d.scalar_tensor_tensor(out=f_row, in0=f_chunk, scalar=-float(S), in1=f_rank,
                                        op0=ALU.mult, op1=ALU.add))
            link(d.tensor_scalar(f_is, f_chunk, 1.0, None, ALU.is_ge))
            link(d.scalar_tensor_tensor(out=f_sum, in0=f_chunk, scalar=float(E - 1), in1=f_over,
                                        op0=ALU.add, op1=ALU.add))
            link(d.tensor_tensor(f_sum, f_sum, top_e[:], ALU.subtract))
            link(d.tensor_tensor(f_sum, f_sum, f_is, ALU.mult))
            d.tensor_tensor(f_col, f_sum, top_e[:], ALU.add).then_inc(place_ready, 1)
            v.wait_ge(place_ready, 1)
            for k in range(K):
                r = slice(k * NT, (k + 1) * NT)
                d.tensor_tensor(col_one[:, r, :], iota[:, 0:NCOL].unsqueeze(1).broadcast_to([P, NT, NCOL]),
                                f_col[:, k, :].unsqueeze(2).broadcast_to([P, NT, NCOL]), ALU.is_equal
                                ).then_inc(col_one_ready, 1)
            for k in range(K):
                d.tensor_tensor(row_hot[k],
                                iota[:, 0:S].unsqueeze(1).broadcast_to([P, NT, S]),
                                f_row[:, k, :].unsqueeze(2).broadcast_to([P, NT, S]), ALU.is_equal
                                ).then_inc(row_hot_ready, 1)
            v.wait_ge(table_done, 1)
            link(d.tensor_scalar(slot_f[:, 0, :], ps_t[0:S, 0, 0:NCOL], 0.0, EMPTY, ALU.is_equal, ALU.mult))
            link(d.scalar_tensor_tensor(out=slot_f[:, 1, :], in0=ps_t[0:S, 0, 0:NCOL], scalar=-1.0,
                                        in1=slot_f[:, 0, :], op0=ALU.add, op1=ALU.add))
            link(d.tensor_scalar(slot_f[:, 2, :], slot_f[:, 1, :], float(T), -float(T), ALU.is_ge,
                                 ALU.mult))
            d.tensor_tensor(gather_at[:], slot_f[:, 1, :], slot_f[:, 2, :], ALU.add).then_inc(slots_ready, 1)
            d.tensor_copy(scatter_at[:], slot_f[:, 1, :]).then_inc(slots_ready, 1)
            link(d.tensor_scalar(over_cmp[:], iota[0:E, 0:NOV], over_end[:, 0:1], None, ALU.is_ge))
            d.tensor_copy(over_count[:], over_base[0:1, E:E + 1]).then_inc(owner_ready, 1)
            v.wait_ge(owner_done, 1)
            d.tensor_scalar(over_expert[:], ps_y[0:1, 0, 0:NOV], float(E - 1), None, ALU.min
                            ).then_inc(owner_ready, 1)

            def rows_lo(e0, u):
                v.wait_ge(xt_hi_done, e0 + u + 1)
                k = u % 2
                d.tensor_tensor(column_part(ht_lo, k), gathered_t(k), column_part(ht_hi, k).bitcast(F32),
                                ALU.subtract
                                ).then_inc(xt_lo_done, 1)

            rows_lo(0, 0)
            rows_lo(0, 1)
            v.wait_ge(mod_landed[GB], 16)
            v.wait_ge(h2_written[0], 16 * (NT // 2))

            def bias(i, j):
                v.wait_ge(bias_done, i * PAIR + PAIR + j + 1)
                v.wait_ge(bias_added, i * PAIR + j + 1)
                d.tensor_tensor(bias_row, ps_y[:, j, :], bc[:, GB, bass.ds(i, 1), :].rearrange(
                    "p a d -> p (a d)"), ALU.mult).then_inc(bias_scaled, 1)

            def step(i, u):
                expert_lo(i, u + 2, (0,))
                rows_lo(i * RING, u + 2)
                expert_lo(i, u + 2, (1,))

            with v.Fori(0, TURNS) as i:
                for u in range(RING):
                    step(i, u)
                    if u - 2 in SHARE_STEPS:
                        bias(i, SHARE_STEPS.index(u - 2))
            for j in range(PAIR):
                bias(TURNS, j)

            count = v.value_load(over_count[0:1, 0:1], min_val=0, max_val=NOV)
            with v.If(count > 0):
                with v.Fori(0, NOV) as q:
                    with v.If(count > q):
                        v.wait_ge(ov_hi, 2 * q + 1)
                        d.tensor_tensor(w_lo[:, 0, :, :], slot3(0), w_hi[:, 0, :, :].bitcast(F32),
                                        ALU.subtract).then_inc(ov_lo, 1)
                        v.wait_ge(ov_hi, 2 * q + 2)
                        d.tensor_tensor(column_part(ht_lo, 0), gathered_t(0),
                                        column_part(ht_hi, 0).bitcast(F32), ALU.subtract).then_inc(ov_lo, 1)
                    with v.Else():
                        v.nop()
                    v.nop()
                v.nop()
            with v.Else():
                v.nop()

            for n in range(NT):
                v.wait_ge(rows_landed[n], 16)
                v.wait_ge(second_ready, n + 1)
                row = raw[:, n, 0:D]
                link(d.scalar_tensor_tensor(out=row, in0=row, scalar=weight[:, 0, n:n + 1],
                                            in1=raw[:, n, D:2 * D], op0=ALU.mult, op1=ALU.add))
                if n < NT - 1:
                    d.tensor_tensor(row, row, bc[:, GB, n // PAIR, :], ALU.mult).then_inc(sum_ready, 1)
                else:
                    link(d.tensor_tensor(row, row, bc[:, GB, n // PAIR, :], ALU.mult))
                    v.wait_ge(bias_added, 1 + NT)
                    d.tensor_tensor(xs[:, n, :], xs[:, n, :], row, ALU.add).then_inc(last_ready, 1)

        @block.gpsimd
        def _(p):
            q7 = nc.gpsimd
            p.sem_inc(half_used, 1)
            p.sem_inc(expert_done, 1)
            p.sem_inc(expert_read, 2)
            p.sem_inc(rows_left, Y_RING)
            p.sem_inc(ov_done, 1)
            p.sem_inc(bias_done, PAIR)
            p.sem_inc(bias_scaled, PAIR)
            p.sem_inc(bias_added, 1)
            q7.memset(half[:], -0.5).then_inc(half_done, 1)
            p.wait_ge(half_done, 1)

            chained = [0]

            def link(ins):
                chained[0] += 1
                ins.then_inc(pool_chain, 1)
                p.wait_ge(pool_chain, chained[0])

            def power(m, out_, n0, n1, done):
                link(q7.tensor_scalar(out_[:, n0:n1], m[:, n0:n1, 1], EPS, None, ALU.add))
                q7.tensor_tensor(out_[:, n0:n1], out_[:, n0:n1], half[:, n0:n1], ALU.pow).then_inc(done, 1)

            p.wait_ge(stats_done, NT // 2)
            power(mv, rstd, 0, NT // 2, rstd_done)
            p.wait_ge(stats_done, NT)
            power(mv, rstd, NT // 2, NT, rstd_done)

            def add_attn(n):
                p.wait_ge(gelu_done, n + 1)
                if n == 0:
                    p.wait_ge(mod_landed[GA], 16)
                row = act[:, n % 2, :]
                link(q7.tensor_tensor(row, row, bc[:, GA, n // PAIR, :], ALU.mult))
                q7.tensor_tensor(xs[:, n, :], xs[:, n, :], row, ALU.add).then_inc(x2_ready, 1)

            def second_rstd(n):
                p.wait_ge(stats2_done, n + 1)
                power(mv2, rstd2, n, n + 1, rstd2_done)

            add_attn(0)
            for n in range(1, NT):
                add_attn(n)
                second_rstd(n - 1)
            second_rstd(NT - 1)

            p.wait_ge(weight_ready, 1)
            for k, dst in enumerate((share, share_tmp)):
                link(q7.tensor_tensor(dst, hot[:, k], weight[:, k, :].unsqueeze(2).broadcast_to([P, NT, E]),
                                      ALU.mult))
            q7.tensor_tensor(share, share, share_tmp, ALU.add).then_inc(share_ready, 1)
            for k in range(K):
                r = slice(k * NT, (k + 1) * NT)
                p.wait_ge(col_one_ready, k + 1)
                q7.tensor_tensor(col_hot[:, r, :], col_one[:, r, :],
                                 pair_id[:, k, :].unsqueeze(2).broadcast_to([P, NT, NCOL]), ALU.mult
                                 ).then_inc(col_hot_ready, 1)

            def gather(at, s, done):
                q7.indirect_dma_start(ring_g[s], None, h2_rows, bass.IndirectOffsetOnAxis(ap=at, axis=0),
                                      bounds_check=T - 1, oob_is_err=False).then_inc(done, 16)

            def scatter(at, rows, done):
                q7.indirect_dma_start(y_rows, bass.IndirectOffsetOnAxis(ap=at, axis=0), rows, None,
                                      bounds_check=K * T - 1, oob_is_err=False).then_inc(done, 16)

            p.wait_ge(h2_written[0], 16 * (NT // 2))
            p.wait_ge(h2_written[1], 16 * (NT // 2))
            p.wait_ge(y_done, NT)
            p.wait_ge(share_t_done, 2)
            p.wait_ge(slots_ready, 2)
            for e in range(AHEAD):
                gather(gather_at[:, e:e + 1], e, gathered[e])

            def add_bias(n):
                p.wait_ge(bias_scaled, PAIR + n + 1)
                q7.tensor_tensor(xs[:, n, :], xs[:, n, :], bias_row, ALU.add).then_inc(bias_added, 1)

            bias_after = {i * RING + u + 2: i * PAIR + j for i in range(TURNS)
                          for j, u in enumerate(SHARE_STEPS)}
            for e in range(E):
                ahead = e + AHEAD
                if ahead < E:
                    if ahead >= RING:
                        p.wait_ge(g_used, ahead - RING + 1)
                    gather(gather_at[:, ahead:ahead + 1], ahead % RING, gathered[ahead % RING])
                if e >= Y_RING - 1:
                    left = e - (Y_RING - 1)
                    p.wait_ge(scattered[left % Y_RING], 16 * (left // Y_RING + 1))
                    p.sem_inc(rows_left, 1)
                p.wait_ge(expert_read, e + 3)
                scatter(scatter_at[:, e:e + 1], ring_y[e % Y_RING], scattered[e % Y_RING])
                if e in bias_after:
                    add_bias(bias_after[e])
            add_bias(NT - 2)

            p.wait_ge(owner_ready, 2)
            count = p.value_load(over_count[0:1, 0:1], min_val=0, max_val=NOV)
            for s in range(Y_RING):
                p.wait_ge(scattered[s], 16 * len(range(s, E, Y_RING)))
            for s in range(RING):
                p.wait_ge(gathered[s], 16 * len(range(s, E, RING)))
            with p.If(count > 0):
                with p.Fori(0, NOV) as q:
                    with p.If(count > q):
                        q7.tensor_copy(over_at[:, 0:1], gather_at[:, bass.ds(q + E, 1)]).then_inc(ov_at, 1)
                        q7.tensor_copy(over_at[:, 1:2], scatter_at[:, bass.ds(q + E, 1)]).then_inc(ov_at, 1)
                        p.wait_ge(ov_at, 2 * q + 2)
                        p.sem_inc(ov_turn, 1)
                        gather(over_at[:, 0:1], 1, ov_g)
                        p.wait_ge(ov_out, q + 1)
                        p.sem_inc(ov_turn, 1)
                        scatter(over_at[:, 1:2], act[0:S, 0, :], scattered[0])
                        p.wait_ge(scattered[0], 16 * q + 16 * (len(range(0, E, Y_RING)) + 1))
                        p.sem_inc(ov_done, 1)
                    with p.Else():
                        p.nop()
                    p.nop()
                p.nop()
            with p.Else():
                p.nop()
            p.sem_inc(rows_complete, 1)

            add_bias(NT - 1)
            p.wait_ge(bias_added, 1 + NT)
            for n in range(NT - 1):
                p.wait_ge(sum_ready, n + 1)
                q7.tensor_tensor(xs[:, n, :], xs[:, n, :], raw[:, n, 0:D], ALU.add).then_inc(out_ready, 1)

        @block.tensor
        def _(pe):
            t_ = nc.tensor

            def product(out_, l_hi, l_lo, r_hi, r_lo, chunks=range(NC)):
                for c in chunks:
                    t_.matmul(out_, l_hi(c), r_hi(c), start=(c == 0), stop=False)
                    t_.matmul(out_, l_hi(c), r_lo(c), start=False, stop=False)
                    ins = t_.matmul(out_, l_lo(c), r_hi(c), start=False, stop=(c == NC - 1))
                return ins

            def mod_row(slot, job):
                pe.wait_ge(raw_landed[slot], 16)
                if job >= 2:
                    pe.wait_ge(m_read, job - 1)
                for c in range(NC):
                    ins = t_.matmul(ps_m[0:NB, job % 2, :], c_silu[:, c, :], slot3(slot)[:, c, :],
                                    start=(c == 0), stop=(c == NC - 1))
                ins.then_inc(m_done, 1)

            def mod_columns(row, job):
                pe.wait_ge(m_read, job - 1)
                for c in range(NC):
                    ins = t_.transpose(ps_m[:, job % 2, c * NB:(c + 1) * NB], row[:, c * P:(c + 1) * P],
                                       ident[0:NB, 0:NB])
                ins.then_inc(m_done, 1)

            def transposes(n):
                pe.wait_ge(norm_ready, n + 1)
                if n < 2:
                    pe.wait_ge(attn_read, n + 1)
                else:
                    pe.wait_ge(ht_ready, NC * (n - 1))
                for c in range(NC):
                    ins = t_.transpose(ps_t[:, n % 2, c * P:(c + 1) * P], norm[:, n % 2, c * P:(c + 1) * P],
                                       ident)
                ins.then_inc(t_done, 1)

            def attention(n):
                pe.wait_ge(ht_lo_done, n + 1)
                if n == 0:
                    pe.wait_ge(attn_lo_done, NC)
                if n >= 2:
                    pe.wait_ge(y_read, n - 1)
                m = slice((n % 2) * P, (n % 2 + 1) * P)
                product(ps_y[:, n % 2, :], lambda c: ht_hi[:, c, m], lambda c: ht_lo[:, c, m],
                        lambda c: attn_hi[:, c, :], lambda c: attn_lo[:, c, :]).then_inc(y_done, 1)

            def transposes2(n):
                pe.wait_ge(h2_ready, n + 1)
                if n < 2:
                    pe.wait_ge(attn_read, NC)
                else:
                    pe.wait_ge(logits_read, n - 1)
                for c in range(NC):
                    ins = t_.transpose(ps_t[:, 2 + n % 2, c * P:(c + 1) * P], h2[:, n % 2, c * P:(c + 1) * P],
                                       ident)
                ins.then_inc(t2_done, 1)

            def logits(n):
                pe.wait_ge(h2t_ready, n + 1)
                for c in range(NC):
                    ins = t_.matmul(ps_t[:, 2 + n % 2, 0:E], g[:, n % 2, c * P:(c + 1) * P], gate[:, c, :],
                                    start=(c == 0), stop=(c == NC - 1))
                ins.then_inc(logits_done, 1)

            def ranks(n0, n1):
                pe.wait_ge(picks_ready, n1)
                o = ps_m[:, 1, n0 * E:n1 * E]
                t_.matmul(o, tri, prod[:, n0:n1, :].rearrange("p n e -> p (n e)"), start=True, stop=False)
                t_.matmul(o, ones, before[:, n0:n1, :].rearrange("p n e -> p (n e)"), start=False, stop=True
                          ).then_inc(ranks_done, n1 - n0)

            for h in range(2):
                pe.wait_ge(lo_ready, SPLIT * (h + 1))
                for c in range(NC):
                    m = slice(c * P, (c + 1) * P)
                    ins = product(ps_t[:, c, :], lambda q: w_hi[:, 0, q, m], lambda q: w_lo[:, 0, q, m],
                                  lambda q: w_hi[:, 1, q, :], lambda q: w_lo[:, 1, q, :],
                                  range(2 * h, 2 * h + 2))
                    if h == 1:
                        ins.then_inc(attn_done, 1)
            pe.wait_ge(silu_done, 1)
            pe.wait_ge(consts_landed, 16)
            mod_row(2, ROW_SA)
            mod_row(3, ROW_CA)
            transposes(0)
            transposes(1)
            mod_columns(row_sa, COL_SA)
            mod_columns(row_ca, COL_CA)
            mod_row(4, ROW[GA])
            attention(0)
            transposes(2)
            attention(1)
            mod_row(5, ROW[SB])
            transposes(3)
            mod_row(6, ROW[CB])
            attention(2)
            transposes(4)
            attention(3)
            mod_row(7, ROW[GB])
            transposes(5)
            attention(4)
            transposes(6)
            attention(5)
            transposes(7)
            attention(6)
            transposes2(0)
            attention(7)
            logits(0)
            transposes2(1)
            logits(1)
            transposes2(2)
            logits(2)
            transposes2(3)
            logits(3)
            transposes2(4)
            logits(4)
            transposes2(5)
            logits(5)
            transposes2(6)
            transposes2(7)
            logits(6)
            logits(7)
            pe.wait_ge(m_read, ROW[GB] + 1)
            ranks(0, 6)
            ranks(6, 8)
            t_.matmul(ps_m[0:E, 0, 0:P], before[:, NT, :], ones, start=True, stop=True
                      ).then_inc(total_done, 1)
            pe.wait_ge(over_ready, 1)
            t_.matmul(ps_m[:, 0, 0:E + 1], over[:], upper, start=True, stop=True)
            t_.matmul(ps_m[0:E, 0, 64:65], upper_inc, over[:, 0:1], start=True, stop=True
                      ).then_inc(base_done, 1)
            pe.wait_ge(share_ready, 1)
            for n in range(NT):
                ins = t_.transpose(ps_t[0:E, 2 + n // 4, (n % 4) * P:(n % 4 + 1) * P], share[:, n, :], ident)
                if n % 4 == 3:
                    ins.then_inc(share_t_done, 1)
            for k in range(K):
                pe.wait_ge(col_hot_ready, k + 1)
                pe.wait_ge(row_hot_ready, k + 1)
                for n in range(NT):
                    r = k * NT + n
                    ins = t_.matmul(ps_t[0:S, 0, 0:NCOL], row_hot[k][:, n, :], col_hot[:, r, :],
                                    start=(r == 0), stop=(r == K * NT - 1))
            ins.then_inc(table_done, 1)
            pe.wait_ge(owner_ready, 1)
            t_.matmul(ps_y[0:1, 0, 0:NOV], ones[0:E, 0:1], over_cmp[:], start=True, stop=True
                      ).then_inc(owner_done, 1)

            def transpose_rows(i, u):
                pe.wait_ge(gathered[u % RING], i * 16 + 16 * (u // RING + 1))
                for c in range(NC):
                    ins = t_.transpose(gathered_t(u % 2)[:, c, :], ring_g[u % RING][:, c * P:(c + 1) * P],
                                       ident[0:S, 0:S])
                ins.then_inc(g_used, 1)

            pe.wait_ge(slots_ready, 2)
            transpose_rows(0, 0)
            pe.wait_ge(owner_ready, 2)
            pe.wait_ge(share_t_read, 2)
            pe.wait_ge(bexp_landed, 16)

            def bias(i, j):
                pe.wait_ge(share_picked, i * PAIR + j + 1)
                pe.wait_ge(bias_scaled, i * PAIR + j + 1)
                t_.matmul(ps_y[:, j, :], share_now[:, j, :], b_exp,
                          start=True, stop=True).then_inc(bias_done, 1)

            def step(i, u, last=False):
                e0 = i * RING
                pe.wait_ge(xt_lo_done, e0 + u + 1)
                if not last:
                    transpose_rows(i, u + 1)
                pe.wait_ge(expert_read, e0 + u + 1)
                k = u % 2
                for h in range(2):
                    pe.wait_ge(lo_ready, e0 * 2 + 2 * (SPLIT + u) + h + 1)
                    product(ps_m[0:S, k, :], lambda c: column_part(ht_hi, k)[:, c, :],
                            lambda c: column_part(ht_lo, k)[:, c, :],
                            lambda c: w_hi[:, k, c, :], lambda c: w_lo[:, k, c, :],
                            range(2 * h, 2 * h + 2)).then_inc((half_used, expert_done)[h], 1)

            with pe.Fori(0, TURNS) as i:
                for u in range(RING):
                    step(i, u)
                    if u - 1 in SHARE_STEPS:
                        bias(i, SHARE_STEPS.index(u - 1))
            for u in range(REST):
                step(TURNS, u, last=(u == REST - 1))
            for j in range(PAIR):
                bias(TURNS, j)

            pe.wait_ge(xt_lo_done, E)
            count = pe.value_load(over_count[0:1, 0:1], min_val=0, max_val=NOV)
            with pe.If(count > 0):
                with pe.Fori(0, NOV) as q:
                    with pe.If(count > q):
                        pe.wait_ge(ov_g, 16 * q + 16)
                        for c in range(NC):
                            ins = t_.transpose(gathered_t(0)[:, c, :], ring_g[1][:, c * P:(c + 1) * P],
                                               ident[0:S, 0:S])
                        ins.then_inc(ov_t, 1)
                        pe.wait_ge(ov_lo, 2 * q + 2)
                        product(ps_m[0:S, 0, :], lambda c: column_part(ht_hi, 0)[:, c, :],
                                lambda c: column_part(ht_lo, 0)[:, c, :],
                                lambda c: w_hi[:, 0, c, :], lambda c: w_lo[:, 0, c, :]).then_inc(ov_y, 1)
                    with pe.Else():
                        pe.nop()
                    pe.nop()
                pe.nop()
            with pe.Else():
                pe.nop()


def _constants():
    import numpy as np
    c = np.zeros((P, C_ALL), np.float32)
    i = np.arange(P)
    c[:, C_ID:C_ID + P] = i[:, None] == i[None, :]
    c[:, C_TRI:C_TRI + P] = i[:, None] < i[None, :]
    c[:, C_ONE:C_ONE + P] = 1
    c[:, C_IOTA:C_IOTA + P] = i[None, :]
    c[0:E, C_UP:C_UP + E] = i[0:E, None] < i[None, 0:E]
    c[0:E, C_UP + E] = 1
    c[0:E, C_INC:C_INC + E] = i[0:E, None] <= i[None, 0:E]
    r = np.arange(K * NT)
    c[:, C_PID:C_PID + K * NT] = r[None, :] * P + i[:, None] + 1
    return c


def kernel(L0_attn_x, L0_attn_w1, L0_attn_w2, L0_attn_b2, L0_attn_sparse_mask, L0_ffn_gate_w,
           L0_ffn_expert_w, L0_ffn_expert_b, L0_c, L0_wmod):
    import numpy as np
    import concourse.bacc as bacc
    from concourse.bass_utils import run_bass_kernel_spmd

    def chunked(a):
        return np.ascontiguousarray(a.reshape(NC, P, -1).transpose(1, 0, 2).reshape(P, -1))

    a = {k: np.asarray(v) for k, v in dict(
        x=L0_attn_x, w1=L0_attn_w1, w2=L0_attn_w2, b2=L0_attn_b2, mask=L0_attn_sparse_mask,
        gate=L0_ffn_gate_w, wexp=L0_ffn_expert_w, bexp=L0_ffn_expert_b, c=L0_c, wmod=L0_wmod).items()}
    arrays = {
        "in_x": a["x"].reshape(T, D),
        "in_w1": a["w1"],
        "in_w2t": np.ascontiguousarray(a["w2"].T),
        "in_b2": a["b2"],
        "in_maskt": chunked(a["mask"].T),
        "in_gatet": chunked(a["gate"].T),
        "in_wexp": np.ascontiguousarray(
            a["wexp"].reshape(E, D, NC, P).transpose(0, 3, 2, 1).reshape(E, P, UNIT)),
        "in_bexp": a["bexp"],
        "in_ct": np.ascontiguousarray(a["c"].T).reshape(P, NC * NB),
        "in_wmod": a["wmod"],
        "in_consts": _constants(),
    }
    nc = bacc.Bacc("TRN2", target_bir_lowering=False, num_devices=1)
    args = [nc.dram_tensor(n, v.shape, mybir.dt.from_np(v.dtype), kind="ExternalInput").ap()
            for n, v in arrays.items()]
    out = nc.dram_tensor("out_0", (NB, PAIR * P, D), F32, kind="ExternalOutput").ap()
    adaln_moe(nc, *args, out)
    r = run_bass_kernel_spmd(nc, [arrays], core_ids=[0])
    return r.results[0]["out_0"]
```
